# Optimizing a Trainium2 kernel written in Bass

```python
import numpy as np
import jax
import jax.numpy as jnp

def _softmax(x, axis=-1):
    return jax.nn.softmax(x, axis=axis)

def _gelu(x):
    return jax.nn.gelu(x, approximate=True)

def _silu(x):
    return jax.nn.silu(x)

def _sigmoid(x):
    return jax.nn.sigmoid(x)

def _layernorm(x, axis=-1, eps=1e-05):
    m = jnp.mean(x, axis=axis, keepdims=True)
    v = jnp.var(x, axis=axis, keepdims=True)
    return (x - m) / jnp.sqrt(v + eps)

def _scatter_add(tgt, idx, src, axis=0):
    return tgt.at[idx].add(src)

def _segment_sum(src, seg, n):
    return jax.ops.segment_sum(src, seg, n)
kernel_name = 'mk_vit_tower_d1_tok_img1024_r4_1ee65d'

def setup_inputs(seed: int=0):
    np.random.seed(seed)
    _w = jnp.asarray

    def _rec_inputs():
        import jax
        import jax.numpy as jnp
        _rk = jax.random.key(seed)
        x = -0.00016672 + 0.999947 * jax.random.normal(jax.random.fold_in(_rk, 1), (16, 3, 96, 96), jnp.float32)
        return x
    x = _rec_inputs()

    def _L0_tok_setup():
        import jax, jax.numpy as jnp
        import numpy as np
        PATCH = 16
        EPS = 1e-05

        def _patchify(x, p):
            B, C, H, W = x.shape
            hp, wp = (H // p, W // p)
            x = x.reshape(B, C, hp, p, wp, p)
            x = x.transpose(0, 2, 4, 1, 3, 5)
            return x.reshape(B, hp * wp, C * p * p)
        key = jax.random.key(seed)
        ks = jax.random.split(key, 6)
        B, C, H = (64, 3, 96)
        E = 256
        P = PATCH
        N = (H // P) ** 2
        D = C * P * P
        x = jax.random.normal(ks[0], (B, C, H, H), dtype=jnp.float32)
        W = jax.random.normal(ks[1], (D, E), dtype=jnp.float32) * (1.0 / np.sqrt(D))
        b = jnp.zeros((E,), dtype=jnp.float32)
        cls_token = jax.random.normal(ks[2], (1, 1, E), dtype=jnp.float32) * 0.02
        pos_embedding = jax.random.normal(ks[3], (1, N + 1, E), dtype=jnp.float32) * 0.02
        gamma = jnp.ones((E,), dtype=jnp.float32)
        beta = jnp.zeros((E,), dtype=jnp.float32)
        return {'x': x, 'W': W, 'b': b, 'cls_token': cls_token, 'pos_embedding': pos_embedding, 'gamma': gamma, 'beta': beta}
    _L0_tok_all = _L0_tok_setup()
    _L0_tok_in = {k: v for k, v in _L0_tok_all.items() if k in ('W', 'b', 'cls_token', 'pos_embedding', 'gamma', 'beta')}
    del _L0_tok_all

    def _L0_attn_setup():
        import jax, jax.numpy as jnp
        import numpy as np
        NUM_HEADS = 16

        def _heads(t, B, L, nh, hd):
            return t.reshape(B, L, nh, hd).transpose(0, 2, 1, 3)

        def _attention(q, k, v, bias):
            hd = q.shape[-1]
            scores = jnp.einsum('bhqd,bhkd->bhqk', q, k) / jnp.sqrt(jnp.float32(hd))
            if bias is not None:
                scores = scores + bias[None, None]
            attn = jax.nn.softmax(scores, axis=-1)
            return jnp.einsum('bhqk,bhkd->bhqd', attn, v)
        key = jax.random.key(seed)
        ks = jax.random.split(key, 5)
        B, L, H = (4, 256, 256)
        s = 0.02
        return {'x': jax.random.normal(ks[0], (B, L, H), jnp.float32), 'Wq': jax.random.normal(ks[1], (H, H), jnp.float32) * s, 'Wkv_short': jax.random.normal(ks[2], (H, 2 * H), jnp.float32) * s, 'Wkv_long': jax.random.normal(ks[3], (H, 2 * H), jnp.float32) * s, 'Wo': jax.random.normal(ks[4], (H, H), jnp.float32) * s, 'mix_weight': jnp.float32(0.5), 'decay_factor': jnp.float32(0.95)}
    _L0_attn_all = _L0_attn_setup()
    _L0_attn_in = {k: v for k, v in _L0_attn_all.items() if k in ('Wq', 'Wkv_short', 'Wkv_long', 'Wo', 'mix_weight', 'decay_factor')}
    del _L0_attn_all

    def _L0_ffn_setup():
        import jax, jax.numpy as jnp
        import numpy as np
        DMODEL = 256
        N_EXPERTS = 32
        EXPERT_SIZE = 128
        N_HEADS = 4
        WEIGHT_SCALE = 1.0
        key = jax.random.key(seed)
        k0, k1, k2, k3 = jax.random.split(key, 4)
        x = jax.random.normal(k0, (2, 512, DMODEL), dtype=jnp.float32)
        expert_sel = jax.random.normal(k1, (N_EXPERTS, DMODEL), dtype=jnp.float32) * DMODEL ** (-0.5)
        keys = jax.random.normal(k2, (N_EXPERTS, DMODEL, EXPERT_SIZE), dtype=jnp.float32) * DMODEL ** (-0.5)
        values = jax.random.normal(k3, (N_EXPERTS, EXPERT_SIZE, DMODEL), dtype=jnp.float32) * (N_EXPERTS * EXPERT_SIZE) ** (-0.5)
        return {'x': x, 'expert_sel': expert_sel, 'keys': keys, 'values': values}
    _L0_ffn_all = _L0_ffn_setup()
    _L0_ffn_in = {k: v for k, v in _L0_ffn_all.items() if k in ('expert_sel', 'keys', 'values')}
    del _L0_ffn_all
    return {'x': x, 'L0_tok_W': _L0_tok_in['W'], 'L0_tok_b': _L0_tok_in['b'], 'L0_tok_cls_token': _L0_tok_in['cls_token'], 'L0_tok_pos_embedding': _L0_tok_in['pos_embedding'], 'L0_tok_gamma': _L0_tok_in['gamma'], 'L0_tok_beta': _L0_tok_in['beta'], 'L0_attn_Wq': _L0_attn_in['Wq'], 'L0_attn_Wkv_short': _L0_attn_in['Wkv_short'], 'L0_attn_Wkv_long': _L0_attn_in['Wkv_long'], 'L0_attn_Wo': _L0_attn_in['Wo'], 'L0_attn_mix_weight': _L0_attn_in['mix_weight'], 'L0_attn_decay_factor': _L0_attn_in['decay_factor'], 'L0_ffn_expert_sel': _L0_ffn_in['expert_sel'], 'L0_ffn_keys': _L0_ffn_in['keys'], 'L0_ffn_values': _L0_ffn_in['values']}

def reference(x, L0_tok_W, L0_tok_b, L0_tok_cls_token, L0_tok_pos_embedding, L0_tok_gamma, L0_tok_beta, L0_attn_Wq, L0_attn_Wkv_short, L0_attn_Wkv_long, L0_attn_Wo, L0_attn_mix_weight, L0_attn_decay_factor, L0_ffn_expert_sel, L0_ffn_keys, L0_ffn_values):
    import jax
    import jax.numpy as jnp

    def _L0_tok_ref(x, W, b, cls_token, pos_embedding, gamma, beta):
        import jax, jax.numpy as jnp
        import numpy as np
        PATCH = 16
        EPS = 1e-05

        def _patchify(x, p):
            B, C, H, W = x.shape
            hp, wp = (H // p, W // p)
            x = x.reshape(B, C, hp, p, wp, p)
            x = x.transpose(0, 2, 4, 1, 3, 5)
            return x.reshape(B, hp * wp, C * p * p)
        B = x.shape[0]
        patches = _patchify(x, PATCH)
        tok = jnp.einsum('bnd,de->bne', patches, W) + b
        cls = jnp.broadcast_to(cls_token, (B, 1, tok.shape[-1]))
        h = jnp.concatenate([cls, tok], axis=1) + pos_embedding
        mu = jnp.mean(h, axis=-1, keepdims=True)
        var = jnp.mean(jnp.square(h - mu), axis=-1, keepdims=True)
        out = (h - mu) * jax.lax.rsqrt(var + EPS) * gamma + beta
        return out

    def _L0_attn_ref(x, Wq, Wkv_short, Wkv_long, Wo, mix_weight, decay_factor):
        import jax, jax.numpy as jnp
        import numpy as np
        NUM_HEADS = 16

        def _heads(t, B, L, nh, hd):
            return t.reshape(B, L, nh, hd).transpose(0, 2, 1, 3)

        def _attention(q, k, v, bias):
            hd = q.shape[-1]
            scores = jnp.einsum('bhqd,bhkd->bhqk', q, k) / jnp.sqrt(jnp.float32(hd))
            if bias is not None:
                scores = scores + bias[None, None]
            attn = jax.nn.softmax(scores, axis=-1)
            return jnp.einsum('bhqk,bhkd->bhqd', attn, v)
        B, L, H = x.shape
        nh = NUM_HEADS
        hd = H // nh
        q = _heads(x @ Wq, B, L, nh, hd)
        kv_s = x @ Wkv_short
        k_s = _heads(kv_s[..., :H], B, L, nh, hd)
        v_s = _heads(kv_s[..., H:], B, L, nh, hd)
        pos = jnp.arange(L, dtype=jnp.float32)
        decay_bias = -jnp.abs(pos[None, :] - pos[:, None]) * (1.0 - decay_factor)
        out_short = _attention(q, k_s, v_s, decay_bias)
        kv_l = x @ Wkv_long
        k_l = _heads(kv_l[..., :H], B, L, nh, hd)
        v_l = _heads(kv_l[..., H:], B, L, nh, hd)
        out_long = _attention(q, k_l, v_l, None)
        alpha = jax.nn.sigmoid(mix_weight)
        out = alpha * out_short + (1.0 - alpha) * out_long
        out = out.transpose(0, 2, 1, 3).reshape(B, L, H)
        return out @ Wo

    def _L0_ffn_ref(x, expert_sel, keys, values):
        import jax, jax.numpy as jnp
        import numpy as np
        DMODEL = 256
        N_EXPERTS = 32
        EXPERT_SIZE = 128
        N_HEADS = 4
        WEIGHT_SCALE = 1.0
        B, S, D = x.shape
        xt = x.reshape(-1, D)
        N = xt.shape[0]
        sel_logits = jnp.einsum('nd,ed->ne', xt, expert_sel)
        gates = jax.nn.sigmoid(sel_logits)
        sel_val, sel_idx = jax.lax.top_k(gates, N_HEADS)
        gate_full = jnp.zeros_like(gates).at[jnp.arange(N)[:, None], sel_idx].set(sel_val)
        scores = jax.nn.relu(jnp.einsum('nd,edf->nef', xt, keys))
        scores = scores * gate_full[:, :, None]
        out = jnp.einsum('nef,efv->nv', scores, values)
        return out.reshape(B, S, -1)
    h = _L0_tok_ref(x, L0_tok_W, L0_tok_b, L0_tok_cls_token, L0_tok_pos_embedding, L0_tok_gamma, L0_tok_beta)
    h = h + _L0_attn_ref(_layernorm(h, axis=-1), L0_attn_Wq, L0_attn_Wkv_short, L0_attn_Wkv_long, L0_attn_Wo, L0_attn_mix_weight, L0_attn_decay_factor)
    h = h + _L0_ffn_ref(_layernorm(h, axis=-1), L0_ffn_expert_sel, L0_ffn_keys, L0_ffn_values)
    return h

_drawn_inputs = setup_inputs


def setup_inputs(seed=0):
    import zlib

    import numpy as np

    out = dict(_drawn_inputs(seed))
    spreads = {'L0_tok_b': (0.0, 0.1), 'L0_tok_gamma': (1.0, 0.2), 'L0_tok_beta': (0.0, 0.1)}
    factors = {'L0_attn_Wq': 8.0, 'L0_attn_Wkv_long': 2.833}
    for name, (base, spread) in spreads.items():
        noise = np.random.default_rng([zlib.crc32(name.encode()), seed]).standard_normal(out[name].shape)
        drawn = base * np.exp(spread * noise) if base else spread * noise
        out[name] = jnp.asarray(drawn.astype(out[name].dtype))
    for name, factor in factors.items():
        out[name] = (out[name] * factor).astype(out[name].dtype)
    return out
```

```python
from contextlib import ExitStack

import concourse.bass as bass
from concourse import mybir

F32 = mybir.dt.float32
F32R = mybir.dt.float32r
BF16 = mybir.dt.bfloat16
ALU = mybir.AluOpType
ACT = mybir.ActivationFunctionType
AX = mybir.AxisListType

P = 128
EPS = 1e-5
HEADS = 16
TOP = 4
Q, KS, KL, VS, VL, WO = range(6)


def vit_tower(nc, x, tok_w, tok_b, cls_token, pos, gamma, beta, wq, wkv_short, wkv_long, wo,
              mix_weight, decay_factor, expert_sel, keys, values, out):
    B, C, IMG, _ = x.shape
    PATCH = 16
    G = IMG // PATCH
    N = G * G + 1
    T = B * N
    D = tok_w.shape[1]
    DK = D // P
    KT = tok_w.shape[0] // P
    BH = B * G
    E, _, F = keys.shape
    HD = D // HEADS
    HH = P // HD
    HQ = HH * N
    HALF = T // 2
    BHALF = B // 2
    N2 = 2 * N
    TILES = [(t, min(P, T - t)) for t in range(0, T, P)]
    NT = len(TILES)
    LAST = TILES[-1][1]
    RING = 4
    assert F == P and HQ == HALF and C * 2 == KT and T % 2 == 0 and HALF % 2 == 0

    with ExitStack() as ctx:
        def sb(name, shape, dt=F32, to=ctx):
            return to.enter_context(nc.sbuf_tensor(name, shape, dt))

        def sem(name):
            return ctx.enter_context(nc.semaphore(name))

        ident = sb("ident", [P, P])
        zeros = sb("zeros", [P, 512], BF16)
        head_mask = sb("head_mask", [P, HH])
        parity = sb("parity", [P, 2])
        neg_half = sb("neg_half", [P, 1])
        bias_t = sb("bias_t", [N2, N])
        dist_i = sb("dist_i", [N2, N], mybir.dt.int32)
        dist = sb("dist", [N2, 2, N])
        scal = sb("scal", [P, 8])
        gam = sb("gam", [P, D])
        bet = sb("bet", [P, D])
        sel_t = [sb(f"sel_t_{p}", [P, DK, P], F32R) for p in ("hi", "lo")]
        h1 = sb("h1", [P, NT, D])
        xn = sb("xn", [P, 2, D])
        stats = sb("stats", [P, 6])
        mv = sb("mv", [P, 3, NT, 2])
        veps = sb("veps", [P, 3, NT])
        rstd = sb("rstd", [P, 3, NT])
        xt = [sb(f"xt_{p}", [P, DK, T], F32R) for p in ("hi", "lo")]
        w_raw = sb("w_raw", [P, DK, 6, D])
        w = [sb(f"w_{p}", [P, DK, 6, D], F32R) for p in ("hi", "lo")]
        raw_k = sb("raw_k", [P, RING, D])
        raw_v = sb("raw_v", [P, RING, D])
        ek = [sb(f"ek_{p}", [P, RING, DK, P], F32R) for p in ("hi", "lo")]
        ev = [sb(f"ev_{p}", [P, RING, D], F32R) for p in ("hi", "lo")]
        early = ExitStack()
        x_in = sb("x_in", [BH, C, PATCH * IMG], to=early)
        x_cols = sb("x_cols", [BH, C, G, PATCH * PATCH], to=early)
        pt = [sb(f"patch_t_{p}", [P, KT, T], F32R, to=early) for p in ("hi", "lo")]
        wt_raw = sb("wt_raw", [P, KT, D], to=early)
        wt = [sb(f"wt_{p}", [P, KT, D], F32R, to=early) for p in ("hi", "lo")]
        pick = sb("pick", [N, B, N], to=early)
        pos_b = sb("pos_b", [N, D], to=early)
        first_rows = sb("first_rows", [N, D], to=early)
        bias_rows = sb("bias_rows", [N, D], to=early)
        sel_raw = sb("sel_raw", [E, D], to=early)
        hg = sb("hg", [P, D], to=early)
        early.close()
        qt = sb("qt", [P, DK, T])
        kt = sb("kt", [P, DK, B, 2, N])
        v_sb = sb("v_sb", [P, 2, 2, D])
        k_now = sb("k_now", [P, 2, DK, N2])
        q_now = sb("q_now", [P, 2, DK, HQ])
        st_sb = sb("st_sb", [N2, 2, HEADS * N])
        probs = sb("probs", [P, 2, NT * N2])
        probs_n = sb("probs_n", [P, 2, NT * N2])
        row_max = sb("row_max", [P, 2 * NT])
        row_sum = sb("row_sum", [P, 2 * NT])
        row_inv = sb("row_inv", [P, 2, 2 * NT])
        pt_sb = sb("pt_sb", [N2, 2, HEADS * N])
        v_now = sb("v_now", [N2, 2, D])
        o_part = sb("o_part", [P, DK, N])
        ot = sb("ot", [P, DK, T])
        o_split = [sb(f"o_{p}", [P, DK, T], F32R) for p in ("hi", "lo")]
        h2 = sb("h2", [P, NT, D])
        gate_e = sb("gate_e", [E, T])
        gate_t = sb("gate_t", [E, T])
        gates = sb("gates", [P, NT, E + TOP])
        gates_rest = sb("gates_rest", [P, NT, E + TOP])
        gates_top = sb("gates_top", [P, NT, E])
        top8 = sb("top8", [P, NT, 8])
        gate_all = sb("gate_all", [P, RING, T])
        relu_h = sb("relu_h", [P, RING, T])
        hg_f = sb("hg_f", [P, 2, T])
        hs = [sb(f"hs_{p}", [P, 2, T], F32R) for p in ("hi", "lo")]
        res = sb("res", [P, 2, D])

        ps = ctx.enter_context(nc.psum_tensor("ps", [P, 8, 512], F32))
        v_dram = nc.dram_tensor("v_rows", [T, 2, D], F32, kind="Internal").ap()
        g_dram = nc.dram_tensor("gate_rows", [E, T], F32, kind="Internal").ap()

        x_landed = [sem(f"x_landed{c}") for c in range(C)]
        wt_landed = [sem(f"wt_landed{c}") for c in range(C)]
        pos_landed, cls_landed, bias_landed, gb_landed, sel_landed, scal_landed = (
            sem(s) for s in ("pos_landed", "cls_landed", "bias_landed", "gb_landed", "sel_landed", "scal_landed"))
        wqk_landed, wv_landed, wo_landed = sem("wqk_landed"), sem("wv_landed"), sem("wo_landed")
        k_landed = [sem(f"k_landed{i}") for i in range(RING)]
        v_landed = [sem(f"v_landed{i}") for i in range(RING)]
        g_landed = [sem(f"g_landed{i}") for i in range(RING)]
        x_sorted, zeros_done = sem("x_sorted"), sem("zeros_done")
        const_done = sem("const_done")
        pool_step = sem("pool_step")
        dve_step = sem("dve_step")
        wt_hi, wt_lo = sem("wt_hi"), sem("wt_lo")
        sel_turned, sel_hi, sel_lo = sem("sel_turned"), sem("sel_hi"), sem("sel_lo")
        patch_turned, patch_hi, patch_lo = sem("patch_turned"), sem("patch_hi"), sem("patch_lo")
        pos_ready = sem("pos_ready")
        bias_ready, mix_exp, mix_ready, parity_ready = sem("bias_ready"), sem("mix_exp"), sem("mix_ready"), sem("parity_ready")
        tok_done = sem("tok_done")
        var_ready, rstd_ready = sem("var_ready"), sem("rstd_ready")
        xn_ready, xn_turned, xt_hi, xt_lo = sem("xn_ready"), sem("xn_turned"), sem("xt_hi"), sem("xt_lo")
        w_split = sem("w_split")
        qk_done, q_out, k_out = sem("qk_done"), sem("q_out"), sem("k_out")
        v_done, v_out = sem("v_done"), [sem("v_out0"), sem("v_out1")]
        v_stored = [sem("v_stored0"), sem("v_stored1")]
        v_loaded = [sem("v_loaded0"), sem("v_loaded1")]
        k_copied, q_masked = sem("k_copied"), sem("q_masked")
        st_done, st_biased, s_turned = sem("st_done"), sem("st_biased"), sem("s_turned")
        max_done, sub_done, exp_done, sum_done, inv_done = (
            sem(s) for s in ("max_done", "sub_done", "exp_done", "sum_done", "inv_done"))
        p_scaled, p_turned, p_copied, pv_done, half_out, o_out = (
            sem(s) for s in ("p_scaled", "p_turned", "p_copied", "pv_done", "half_out", "o_out"))
        s_cleared = sem("s_cleared")
        o_hi, o_lo, wo_done = sem("o_hi"), sem("o_lo"), sem("wo_done")
        h2_ready, x2_turned, x2_hi, x2_lo = sem("h2_ready"), sem("x2_turned"), sem("x2_hi"), sem("x2_lo")
        logit_done, gate_exp, gate_sig, gate_turned, gate_top, gate_back, gate_out, gate_stored = (
            sem(s) for s in ("logit_done", "gate_exp", "gate_sig", "gate_turned", "gate_top", "gate_back",
                             "gate_out", "gate_stored"))
        gate_cleared = sem("gate_cleared")
        k_split, v_split = sem("k_split"), sem("v_split")
        ek_hi, ev_hi = sem("ek_hi"), sem("ev_hi")
        up_done, relu_done, gated, h_hi, h_lo, down_done = (
            sem(s) for s in ("up_done", "relu_done", "gated", "h_hi", "h_lo", "down_done"))
        tile_done, res_ready = sem("tile_done"), sem("res_ready")
        out_stored = [sem("out_stored0"), sem("out_stored1")]

        def f32(ap):
            return ap.bitcast(F32)

        WG = G // 2

        def patch_view(t, k, g):
            v = t[:, k, :].rearrange("p (b n) -> p b n", n=N)[:, :, 1:N]
            return v.rearrange("p b (h w) -> p w b h", w=G)[:, WG * g:WG * g + WG]

        def patch_psum(bank):
            return ps[:, bank, 0:WG * BH].rearrange("p (w b h) -> p w b h", w=WG, b=B)

        st_ps = ps[0:N2, 0:2, 0:HQ]
        pt_ps = ps[:, 4:6, :].rearrange("p a n -> p (a n)")[0:N2, 0:HEADS * N]

        def s_ps(slot):
            return ps[:, 2 + slot, 0:NT * N2]

        def o_ps(slot):
            return ps[:, 6 + slot, 0:DK * N2]

        def down_ps(i):
            return ps[:, 4 + i // 2, (i % 2) * D:(i % 2) * D + D]

        block = ctx.enter_context(nc.Block())

        @block.sync
        def _(sp):
            for c in range(C):
                x_c = bass.AP(x.tensor, x.offset + c * IMG * IMG,
                              [[C * IMG * IMG, B], [PATCH * IMG, G], [1, PATCH * IMG]])
                sp.dma_start(x_in[:, c, :], x_c).then_inc(x_landed[c], 16)
            sp.dma_start(w_raw[:, :, Q, :], wq.rearrange("(k p) n -> p k n", p=P)).then_inc(wqk_landed, 16)
            for n, src in ((KS, wkv_short), (KL, wkv_long)):
                sp.dma_start(w_raw[:, :, n, :], src[:, 0:D].rearrange("(k p) n -> p k n", p=P)).then_inc(wqk_landed, 16)
            for n, src in ((VS, wkv_short), (VL, wkv_long)):
                sp.dma_start(w_raw[:, :, n, :], src[:, D:2 * D].rearrange("(k p) n -> p k n", p=P)).then_inc(wv_landed, 16)
            sp.dma_start(w_raw[:, :, WO, :], wo.rearrange("(k p) n -> p k n", p=P)).then_inc(wo_landed, 16)

            def load_keys(e, slot):
                sp.dma_start(raw_k[:, slot, :].rearrange("p (k f) -> p k f", k=DK),
                             keys[bass.ds(e, 1)].rearrange("o (k p) f -> p (o k) f", p=P)).then_inc(k_landed[slot], 16)

            def load_values(e, slot):
                sp.dma_start(raw_v[:, slot, :],
                             values[bass.ds(e, 1)].rearrange("o p n -> p (o n)")).then_inc(v_landed[slot], 16)

            for e in range(RING):
                load_keys(e, e)
                load_values(e, e)
            for e in range(RING, 2 * RING):
                sp.wait_ge(k_split, e - RING + 1)
                load_keys(e, e - RING)
                sp.wait_ge(v_split, e - RING + 1)
                load_values(e, e - RING)

            for i, (t0, n) in enumerate(TILES):
                sp.wait_ge(v_out[i % 2], i // 2 + 1)
                sp.dma_start(v_dram[t0:t0 + n], v_sb[0:n, i % 2]).then_inc(v_stored[i % 2], 16)
            sp.wait_ge(v_stored[0], 16 * ((NT + 1) // 2))
            sp.wait_ge(v_stored[1], 16 * (NT // 2))

            def load_v(b, slot):
                for n in range(2):
                    sp.dma_start(v_now[n * N:(n + 1) * N, slot, :],
                                 v_dram[bass.ds(b * N, N), n, :]).then_inc(v_loaded[slot], 16)

            load_v(0, 0)
            load_v(1, 1)
            with sp.Fori(2, B - 1, 2) as b:
                for u in range(2):
                    sp.wait_ge(pv_done, b + u - 1)
                    load_v(b + u, u)

            sp.wait_ge(gate_out, 1)
            sp.dma_start(g_dram, gate_t[:, :]).then_inc(gate_stored, 16)
            sp.wait_ge(gate_stored, 16)

            def load_gate(e, slot):
                row = g_dram[bass.ds(e, 1), :]
                sp.dma_start(gate_all[:, slot, :], row.to_broadcast([P, T])).then_inc(g_landed[slot], 16)

            for e in range(RING):
                load_gate(e, e)
            with sp.Fori(RING, E - 2 * RING + 1, RING) as e:
                for u in range(RING):
                    sp.wait_ge(gated, e + (u - RING + 1))
                    load_gate(e + u, u)
                    sp.wait_ge(k_split, e + (u + 1))
                    load_keys(e + (u + RING), u)
                    sp.wait_ge(v_split, e + (u + 1))
                    load_values(e + (u + RING), u)
            for e in range(E - RING, E):
                sp.wait_ge(gated, e - RING + 1)
                load_gate(e, e % RING)

            for i, (t0, n) in enumerate(TILES):
                sp.wait_ge(res_ready, i + 1)
                sp.dma_start(out[t0:t0 + n, :], res[0:n, i % 2, :]).then_inc(out_stored[i % 2], 16)
            sp.wait_ge(out_stored[0], 16 * ((NT + 1) // 2))
            sp.wait_ge(out_stored[1], 16 * (NT // 2))

        @block.scalar
        def _(act):
            act.dma_start(sel_raw[:, :], expert_sel).then_inc(sel_landed, 16)
            w_rows = tok_w.rearrange("(k p) n -> p k n", p=P)
            for c in range(C):
                act.dma_start(wt_raw[:, 2 * c:2 * c + 2, :], w_rows[:, 2 * c:2 * c + 2, :]).then_inc(wt_landed[c], 16)
            act.dma_start(pos_b[:, :], pos.rearrange("o n d -> (o n) d")).then_inc(pos_landed, 16)
            act.dma_start(bias_rows[:, :], tok_b.rearrange("(o d) -> o d", o=1).to_broadcast([N, D])).then_inc(bias_landed, 16)
            act.dma_start(first_rows[0:1, :], cls_token.rearrange("o n d -> (o n) d")).then_inc(cls_landed, 16)
            act.dma_start(scal[:, 0:1], mix_weight.rearrange("(o d) -> o d", o=1).to_broadcast([P, 1])).then_inc(scal_landed, 16)
            act.dma_start(scal[:, 1:2], decay_factor.rearrange("(o d) -> o d", o=1).to_broadcast([P, 1])).then_inc(scal_landed, 16)
            act.dma_start(gam[:, :], gamma.rearrange("(o d) -> o d", o=1).to_broadcast([P, D])).then_inc(gb_landed, 16)
            act.dma_start(bet[:, :], beta.rearrange("(o d) -> o d", o=1).to_broadcast([P, D])).then_inc(gb_landed, 16)

            act.wait_ge(zeros_done, 1)
            act.wait_ge(sel_turned, 1)
            act.activation(sel_t[0][:, :, 0:E], ps[:, 7, 0:DK * E].rearrange("p (k e) -> p k e", k=DK), ACT.Copy).then_inc(sel_hi, 1)
            for c in range(C):
                act.wait_ge(wt_landed[c], 16)
                act.activation(wt[0][:, 2 * c:2 * c + 2, :], wt_raw[:, 2 * c:2 * c + 2, :], ACT.Copy).then_inc(wt_hi, 1)
            for g in range(2 * KT):
                act.wait_ge(patch_turned, g + 1)
                act.activation(patch_view(pt[0], g // 2, g % 2), patch_psum(g % 3), ACT.Copy).then_inc(patch_hi, 1)

            def high_keys(e, low, u):
                act.wait_ge(k_landed[u], 4 * e + (16 - 4 * u))
                if low >= RING:
                    act.wait_ge(up_done, e - (RING - 1))
                act.activation(ek[0][:, u], raw_k[:, u, :].rearrange("p (k f) -> p k f", k=DK), ACT.Copy).then_inc(ek_hi, 1)

            def high_values(e, low, u):
                act.wait_ge(v_landed[u], 4 * e + (16 - 4 * u))
                if low >= RING:
                    act.wait_ge(down_done, e - (RING - 1))
                act.activation(ev[0][:, u], raw_v[:, u], ACT.Copy).then_inc(ev_hi, 1)

            for e in range(RING):
                high_keys(e, e, e)
                high_values(e, e, e)
            act.wait_ge(scal_landed, 32)
            act.activation(scal[:, 2:3], scal[:, 0:1], ACT.Exp, scale=-1.0).then_inc(mix_exp, 1)

            for i, (t0, n) in enumerate(TILES):
                act.wait_ge(xn_turned, i + 1)
                act.activation(xt[0][:, :, t0:t0 + n], ps[:, i % 2, 0:DK * P].rearrange("p (k t) -> p k t", k=DK)[:, :, 0:n],
                               ACT.Copy).then_inc(xt_hi, 1)
            for h in range(DK):
                act.wait_ge(qk_done, h + 1)
                act.activation(qt[:, h, :].rearrange("p (c t) -> p c t", c=2), ps[:, 2 * h:2 * h + 2, 0:HALF],
                               ACT.Copy, scale=float(HD) ** -0.5).then_inc(q_out, 1)
            act.wait_ge(mix_ready, 1)
            for i in range(0, NT, 2):
                n = TILES[i][1]
                act.wait_ge(v_done, i + 1)
                if i >= 2:
                    act.wait_ge(v_stored[0], 16 * (i // 2))
                for br in range(2):
                    last = act.activation(v_sb[0:n, 0, br, :], ps[0:n, 6, br * D:(br + 1) * D], ACT.Copy,
                                          scale=scal[0:n, 4 + br:5 + br])
                last.then_inc(v_out[0], 1)
            act.wait_ge(k_out, 4)

            def copy_keys(b, low, slot):
                if low >= 2:
                    act.wait_ge(st_done, b - 1)
                act.activation(k_now[:, slot], kt[:, :, bass.ds(b, 1)].rearrange("p k o n m -> p k (o n m)"),
                               ACT.Copy).then_inc(k_copied, 1)

            def exps(b, slot):
                act.wait_ge(sub_done, b + 1)
                act.activation(probs[:, slot, :], probs[:, slot, :], ACT.Exp).then_inc(exp_done, 1)

            def copy_probs(b, low, slot):
                act.wait_ge(p_turned, b + 1)
                if low >= 2:
                    act.wait_ge(pv_done, b - 1)
                act.activation(pt_sb[:, slot, :], pt_ps, ACT.Copy).then_inc(p_copied, 1)

            def step(s, low, high, u):
                if high + 1 < B:
                    copy_keys(s + 1, low + 1, (u + 1) % 2)
                if low >= 1 and high <= B:
                    exps(s - 1, (u + 1) % 2)
                if low >= 3 and high <= B + 2:
                    copy_probs(s - 3, low - 3, (u + 1) % 2)

            copy_keys(0, 0, 0)
            for s in range(6):
                step(s, s, s, s % 2)
            with act.Fori(6, B - 3, 2) as s:
                for u in range(2):
                    step(s + u, 6, B - 3, u)
            for s in range(B - 2, B + 4):
                step(s, s, s, s % 2)

            for i, (t0, n) in enumerate(TILES):
                act.wait_ge(o_out, min(B, -(-(t0 + n) // N)))
                act.activation(o_split[0][:, :, t0:t0 + n], ot[:, :, t0:t0 + n], ACT.Copy).then_inc(o_hi, 1)
            for i, (t0, n) in enumerate(TILES):
                act.wait_ge(x2_turned, i + 1)
                act.activation(xt[0][:, :, t0:t0 + n], ps[:, 4 + i % 2, 0:DK * P].rearrange("p (k t) -> p k t", k=DK)[:, :, 0:n],
                               ACT.Copy).then_inc(x2_hi, 1)
            act.wait_ge(logit_done, 1)
            act.activation(gate_e[:, :].rearrange("p (c t) -> p c t", c=2), ps[0:E, 6:8, 0:HALF], ACT.Exp,
                           scale=-1.0).then_inc(gate_exp, 1)

            def relu(e, low, u):
                act.wait_ge(up_done, e + 1)
                if low >= RING:
                    act.wait_ge(gated, e - (RING - 1))
                act.activation(relu_h[:, u, :].rearrange("p (c t) -> p c t", c=2),
                               ps[:, 2 * (u % 2):2 * (u % 2) + 2, 0:HALF], ACT.Relu).then_inc(relu_done, 1)

            def high_part(e, low, u):
                act.wait_ge(gated, e + 1)
                if low >= 2:
                    act.wait_ge(down_done, e - 1)
                act.activation(hs[0][:, u, :], hg_f[:, u, :], ACT.Copy).then_inc(h_hi, 1)

            for e in range(RING):
                relu(e, e, e)
                if e >= 2:
                    high_part(e - 2, e - 2, e % 2)
                    high_keys(e + 2, e + 2, e - 2)
            with act.Fori(RING, E - 2 * RING + 1, RING) as e:
                for u in range(RING):
                    relu(e + u, RING, u)
                    high_part(e + (u - 2), 2, u % 2)
                    high_keys(e + (u + 2), RING, (u + 2) % RING)
                    high_values(e + u, RING, u)
            for e in range(E - RING, E):
                relu(e, e, e % RING)
                high_part(e - 2, e - 2, e % 2)
                if e + 2 < E:
                    high_keys(e + 2, e + 2, (e + 2) % RING)
                high_values(e, e, e % RING)
            for e in range(E - 2, E):
                high_part(e, e, e % 2)

        @block.tensor
        def _(pe):
            def three(dst, stat, mov, first, last, **kw):
                pe.matmul(dst, stat[0], mov[0], start=first, stop=False, **kw)
                pe.matmul(dst, stat[0], mov[1], start=False, stop=False, **kw)
                return pe.matmul(dst, stat[1], mov[0], start=False, stop=last, **kw)

            pe.wait_ge(const_done, 2)
            pe.wait_ge(sel_landed, 16)
            for k in range(DK):
                mm = pe.transpose(ps[:, 7, k * E:(k + 1) * E], sel_raw[:, k * P:(k + 1) * P], ident[0:E, 0:E])
            mm.then_inc(sel_turned, 1)

            def turn_patches(c):
                pe.wait_ge(x_sorted, c + 1)
                for g in range(4 * c, 4 * c + 4):
                    if g >= 3:
                        pe.wait_ge(patch_lo, g - 2)
                    r0 = P * ((g // 2) % 2)
                    for j in range(WG):
                        mm = pe.transpose(ps[:, g % 3, j * BH:(j + 1) * BH],
                                          x_cols[:, c, WG * (g % 2) + j, r0:r0 + P], ident[0:BH, 0:BH])
                    mm.then_inc(patch_turned, 1)

            def embed(c):
                pe.wait_ge(wt_lo, c + 1)
                pe.wait_ge(patch_lo, 4 * c + 4)
                for i, (t0, n) in enumerate(TILES):
                    dst = ps[0:n, 3 + i, 0:D]
                    if c == 0:
                        pe.matmul(dst, pick[:].rearrange("p b n -> p (b n)")[:, t0:t0 + n], pos_b[:, :], start=True, stop=False)
                    for k in (2 * c, 2 * c + 1):
                        mm = three(dst, [a[:, k, t0:t0 + n] for a in pt], [a[:, k, :] for a in wt], False, k == KT - 1)
                    if c == C - 1:
                        mm.then_inc(tok_done, 1)

            turn_patches(0)
            turn_patches(1)
            pe.wait_ge(const_done, 3)
            pe.wait_ge(pos_ready, 1)
            pe.wait_ge(sel_lo, 1)
            embed(0)
            turn_patches(2)
            embed(1)
            embed(2)

            def turn_rows(bank, i, n, done):
                pe.wait_ge(xn_ready, i + 1)
                for k in range(DK):
                    mm = pe.transpose(ps[:, bank, k * P:k * P + n], xn[0:n, i % 2, k * P:(k + 1) * P], ident[0:n, 0:n])
                mm.then_inc(done, 1)

            for i, (t0, n) in enumerate(TILES):
                if i >= 2:
                    pe.wait_ge(xt_lo, i - 1)
                turn_rows(i % 2, i, n, xn_turned)

            pe.wait_ge(w_split, 1)
            pe.wait_ge(xt_lo, NT)
            for j in range(3 * DK):
                kind, h = j // DK, j % DK
                if j == 3:
                    pe.wait_ge(q_out, 1)
                if j == 4:
                    pe.wait_ge(q_out, 2)
                if j == 5:
                    pe.wait_ge(k_out, 1)
                for k in range(DK):
                    for c in range(2):
                        mm = three(ps[:, 2 * (j % 3) + c, 0:HALF], [a[:, k, kind, h * P:(h + 1) * P] for a in w],
                                   [a[:, k, c * HALF:(c + 1) * HALF] for a in xt], k == 0, k == DK - 1)
                mm.then_inc(qk_done, 1)
            pe.wait_ge(w_split, 2)
            for i, (t0, n) in enumerate(TILES):
                if i >= 2:
                    pe.wait_ge(v_out[i % 2], i // 2)
                for k in range(DK):
                    mm = three(ps[0:n, 6 + i % 2, :], [a[:, k, t0:t0 + n] for a in xt],
                               [a[:, k, VS:VL + 1, :] for a in w], k == 0, k == DK - 1)
                mm.then_inc(v_done, 1)

            pe.wait_ge(k_out, 4)
            pe.wait_ge(s_cleared, 1)

            def scores(b, low, u):
                pe.wait_ge(q_masked, b + 1)
                pe.wait_ge(k_copied, b + 1)
                if low >= 1:
                    pe.wait_ge(st_biased, b)
                for h in range(DK):
                    mm = pe.matmul(st_ps[:, h, :], k_now[:, u, h, :], q_now[:, u, h, :], start=True, stop=True)
                mm.then_inc(st_done, 1)

            def turn_scores(b, low, u):
                pe.wait_ge(st_biased, b + 1)
                if low >= 2:
                    pe.wait_ge(sub_done, b - 1)
                for i, (t0, n) in enumerate(TILES):
                    mm = pe.transpose(s_ps(u)[0:n, i * N2:(i + 1) * N2], st_sb[:, u, t0:t0 + n], ident[0:N2, 0:N2])
                mm.then_inc(s_turned, 1)

            def turn_probs(b, low, u):
                pe.wait_ge(p_scaled, b + 1)
                if low >= 1:
                    pe.wait_ge(p_copied, b)
                for i, (t0, n) in enumerate(TILES):
                    mm = pe.transpose(pt_ps[:, t0:t0 + n], probs_n[0:n, u, i * N2:(i + 1) * N2], ident[0:n, 0:n])
                mm.then_inc(p_turned, 1)

            def weigh_values(b, low, u):
                pe.wait_ge(p_copied, b + 1)
                pe.wait_ge(v_loaded[u], 16 * b + (32 - 16 * u))
                if low >= 2:
                    pe.wait_ge(o_out, b - 1)
                for h in range(DK):
                    for j in range(HH // 2):
                        pair = h * (HH // 2) + j
                        mm = pe.matmul(o_ps(u)[32 * j:32 * j + 32, h * N2:(h + 1) * N2], v_now[:, u, 32 * pair:32 * pair + 32],
                                       pt_sb[:, u, pair * N2:(pair + 1) * N2], start=True, stop=True)
                mm.then_inc(pv_done, 1)

            def step(s, low, high, u):
                if high < B:
                    scores(s, low, u)
                if low >= 1 and high <= B:
                    turn_scores(s - 1, low - 1, (u + 1) % 2)
                if low >= 3 and high <= B + 2:
                    turn_probs(s - 3, low - 3, (u + 1) % 2)
                if low >= 4 and high <= B + 3:
                    weigh_values(s - 4, low - 4, u)

            for s in range(6):
                step(s, s, s, s % 2)
            with pe.Fori(6, B - 3, 2) as s:
                for u in range(2):
                    step(s + u, 6, B - 3, u)
            for s in range(B - 2, B + 4):
                step(s, s, s, s % 2)

            def project(i, t0, n):
                pe.wait_ge(o_lo, i + 1)
                if i >= 4:
                    pe.wait_ge(h2_ready, i - 3)
                for k in range(DK):
                    mm = three(ps[0:n, i % 4, 0:D], [a[:, k, t0:t0 + n] for a in o_split],
                               [a[:, k, WO, :] for a in w], k == 0, k == DK - 1)
                mm.then_inc(wo_done, 1)

            pe.wait_ge(w_split, 3)
            for i, (t0, n) in enumerate(TILES):
                project(i, t0, n)
            for i, (t0, n) in enumerate(TILES):
                if i >= 2:
                    pe.wait_ge(x2_lo, i - 1)
                pe.wait_ge(xn_ready, NT + i + 1)
                for k in range(DK):
                    mm = pe.transpose(ps[:, 4 + i % 2, k * P:k * P + n], xn[0:n, (NT + i) % 2, k * P:(k + 1) * P], ident[0:n, 0:n])
                mm.then_inc(x2_turned, 1)
            pe.wait_ge(x2_lo, NT)
            for c in range(2):
                for k in range(DK):
                    mm = three(ps[:, 6 + c, 0:HALF], [a[:, k, :] for a in sel_t],
                               [a[:, k, c * HALF:(c + 1) * HALF] for a in xt], k == 0, k == DK - 1)
            mm.then_inc(logit_done, 1)

            def expert_up(e, low, u):
                pe.wait_ge(k_split, e + 1)
                if low >= 2:
                    pe.wait_ge(relu_done, e - 1)
                for k in range(DK):
                    for c in range(2):
                        mm = three(ps[:, 2 * (u % 2) + c, 0:HALF], [a[:, u, k, :] for a in ek],
                                   [a[:, k, c * HALF:(c + 1) * HALF] for a in xt], k == 0, k == DK - 1)
                mm.then_inc(up_done, 1)

            def expert_down(e, u, last):
                pe.wait_ge(h_lo, e + 1)
                pe.wait_ge(v_split, e + 1)
                for i, (t0, n) in enumerate(TILES):
                    mm = three(down_ps(i)[0:n], [a[:, u % 2, t0:t0 + n] for a in hs], [a[:, u, :] for a in ev],
                               False, last, skip_group_check=True)
                    if last:
                        mm.then_inc(tile_done, 1)
                if not last:
                    mm.then_inc(down_done, 1)

            pe.wait_ge(h2_ready, NT)
            expert_up(0, 0, 0)
            expert_up(1, 1, 1)
            pe.wait_ge(gate_sig, 1)
            for i, (t0, n) in enumerate(TILES):
                mm = pe.transpose(ps[0:n, 4, i * E:(i + 1) * E], gate_t[:, t0:t0 + n], ident[0:E, 0:E])
            mm.then_inc(gate_turned, 1)
            expert_up(2, 2, 2)
            pe.wait_ge(gate_top, 1)
            for i, (t0, n) in enumerate(TILES):
                mm = pe.transpose(ps[:, 6:8, :].rearrange("p a n -> p (a n)")[0:E, t0:t0 + n], gates_top[0:n, i, :], ident[0:n, 0:n])
            mm.then_inc(gate_back, 1)
            expert_up(3, 3, 3)
            pe.wait_ge(gate_out, 1)
            for i in range((NT + 1) // 2):
                pe.matmul(ps[:, 4 + i, :], zeros[:, 0:P], zeros[:, :], start=True, stop=False, skip_group_check=True)
            with pe.Fori(RING, E - RING + 1, RING) as e:
                for u in range(RING):
                    expert_up(e + u, RING, u)
                    expert_down(e + (u - RING), u, False)
            for e in range(E - RING, E):
                expert_down(e, e % RING, e == E - 1)

        @block.vector
        def _(dve):
            count = [0]

            def chain(ins):
                count[0] += 1
                ins.then_inc(dve_step, 1)
                dve.wait_ge(dve_step, count[0])

            dve.memset(f32(sel_t[0][:]), 0.0)
            dve.memset(f32(sel_t[1][:]), 0.0)
            dve.memset(zeros[:], 0.0)
            for a in pt:
                last = dve.memset(f32(a[:].rearrange("p k (b n) -> p k b n", n=N)[:, :, :, 0]), 0.0)
            last.then_inc(zeros_done, 1)

            dve.wait_ge(cls_landed, 16)
            dve.wait_ge(bias_landed, 16)
            dve.wait_ge(pos_landed, 16)
            chain(dve.tensor_copy(bias_rows[0:1, :], first_rows[0:1, :]))
            dve.tensor_tensor(pos_b[:, :], pos_b[:, :], bias_rows[:, :], ALU.add).then_inc(pos_ready, 1)
            dve.wait_ge(sel_hi, 1)
            dve.tensor_tensor(sel_t[1][:, :, 0:E], ps[:, 7, 0:DK * E].rearrange("p (k e) -> p k e", k=DK),
                              f32(sel_t[0][:, :, 0:E]), ALU.subtract).then_inc(sel_lo, 1)

            def patch_rest(c):
                for g in range(4 * c, 4 * c + 4):
                    dve.wait_ge(patch_hi, g + 1)
                    dve.tensor_tensor(patch_view(pt[1], g // 2, g % 2), patch_psum(g % 3),
                                      f32(patch_view(pt[0], g // 2, g % 2)), ALU.subtract).then_inc(patch_lo, 1)

            for c in range(C):
                dve.wait_ge(x_landed[c], 16)
                dve.tensor_copy(x_cols[:, c].rearrange("p w (r q) -> p w r q", q=PATCH),
                                x_in[:, c, :].rearrange("p (r w q) -> p w r q", r=PATCH, w=G)).then_inc(x_sorted, 1)
            for c in range(C):
                dve.wait_ge(wt_hi, c + 1)
                dve.tensor_tensor(wt[1][:, 2 * c:2 * c + 2, :], wt_raw[:, 2 * c:2 * c + 2, :],
                                  f32(wt[0][:, 2 * c:2 * c + 2, :]), ALU.subtract).then_inc(wt_lo, 1)
            for c in range(C):
                patch_rest(c)

            dve.wait_ge(const_done, 6)
            dve.wait_ge(scal_landed, 32)
            chain(dve.tensor_copy(dist[:, 0, :], dist_i[:, :]))
            chain(dve.tensor_scalar(dist[:, 1, :], dist[:, 0, :], -1.0, None, ALU.mult))
            chain(dve.tensor_tensor(dist[:, 0, :], dist[:, 0, :], dist[:, 1, :], ALU.max))
            chain(dve.tensor_scalar(scal[:, 3:4], scal[:, 1:2], -1.0, 1.0, ALU.mult, ALU.add))
            dve.tensor_scalar(dist[:, 1, :], dist[:, 0, :], -1.0, scal[0:N2, 3:4], ALU.mult, ALU.mult).then_inc(bias_ready, 1)
            dve.wait_ge(mix_exp, 1)
            chain(dve.tensor_scalar(scal[:, 6:7], scal[:, 2:3], 1.0, None, ALU.add))
            chain(dve.reciprocal(scal[:, 4:5], scal[:, 6:7]))
            chain(dve.tensor_scalar(scal[:, 5:6], scal[:, 4:5], -1.0, 1.0, ALU.mult, ALU.add))
            dve.tensor_reduce(parity[:, :], head_mask[:, :].rearrange("p (j t) -> p t j", t=2), AX.X, ALU.add).then_inc(mix_ready, 1)
            dve.wait_ge(gb_landed, 32)

            made = [0]

            def moments(which, i, src):
                if made[0]:
                    dve.wait_ge(var_ready, made[0])
                made[0] += 1
                chain(dve.bn_stats(stats[0:src.shape[0], :], src))
                dve.bn_aggr(mv[0:src.shape[0], which, i, :], stats[0:src.shape[0], :]).then_inc(var_ready, 1)

            def normed(which, i, n, rstd_seen, src, slot, turned, seen):
                dve.wait_ge(rstd_ready, rstd_seen)
                if seen >= 1:
                    dve.wait_ge(turned, seen)
                dve.tensor_scalar(xn[0:n, slot, :], src, mv[0:n, which, i, 0:1], rstd[0:n, which, i:i + 1],
                                  ALU.subtract, ALU.mult).then_inc(xn_ready, 1)

            order = []
            for s in range(NT + 3):
                if s < NT:
                    t0, n = TILES[s]
                    dve.wait_ge(tok_done, s + 1)
                    moments(0, s, ps[0:n, 3 + s, 0:D])
                    order.append((0, s))
                if 0 <= s - 1 < NT:
                    i = s - 1
                    t0, n = TILES[i]
                    dve.wait_ge(rstd_ready, order.index((0, i)) + 1)
                    chain(dve.scalar_tensor_tensor(hg[0:n, :], ps[0:n, 3 + i, 0:D], mv[0:n, 0, i, 0:1], gam[0:n, :],
                                                   ALU.subtract, ALU.mult))
                    chain(dve.scalar_tensor_tensor(h1[0:n, i, :], hg[0:n, :], rstd[0:n, 0, i:i + 1], bet[0:n, :],
                                                   ALU.mult, ALU.add))
                    moments(1, i, h1[0:n, i, :])
                    order.append((1, i))
                if 0 <= s - 2 < NT:
                    i = s - 2
                    normed(1, i, TILES[i][1], order.index((1, i)) + 1, h1[0:TILES[i][1], i, :], i % 2, xn_turned, i - 1)
                if 0 <= s - 3 < NT:
                    i = s - 3
                    t0, n = TILES[i]
                    dve.wait_ge(xt_hi, i + 1)
                    dve.tensor_tensor(xt[1][:, :, t0:t0 + n],
                                      ps[:, i % 2, 0:DK * P].rearrange("p (k t) -> p k t", k=DK)[:, :, 0:n],
                                      f32(xt[0][:, :, t0:t0 + n]), ALU.subtract).then_inc(xt_lo, 1)

            for j in range(DK, 3 * DK):
                kind, h = j // DK - 1, j % DK
                dve.wait_ge(qk_done, j + 1)
                dve.tensor_copy(kt[:, h, :, kind, :].rearrange("p (c b) n -> p c b n", c=2),
                                ps[:, 2 * (j % 3):2 * (j % 3) + 2, 0:HALF].rearrange("p c (b n) -> p c b n", n=N)).then_inc(k_out, 1)
            for i in range(1, NT, 2):
                n = TILES[i][1]
                dve.wait_ge(v_done, i + 1)
                if i >= 2:
                    dve.wait_ge(v_stored[1], 16 * (i // 2))
                for br in range(2):
                    last = dve.tensor_scalar(v_sb[0:n, 1, br, :], ps[0:n, 7, br * D:(br + 1) * D],
                                             scal[0:n, 4 + br:5 + br], None, ALU.mult)
                last.then_inc(v_out[1], 1)
            dve.memset(ps[:, 2:4, :], 0.0).then_inc(s_cleared, 1)
            dve.wait_ge(const_done, 7)

            def add_bias(b, low, u):
                dve.wait_ge(st_done, b + 1)
                if low >= 2:
                    dve.wait_ge(s_turned, b - 1)
                dve.tensor_tensor(st_sb[:, u, :].rearrange("p (c h n) -> p c h n", c=DK, n=N),
                                  st_ps.rearrange("p c (h n) -> p c h n", n=N),
                                  bias_t[:, :].rearrange("p (a o n) -> p a o n", a=1, o=1).to_broadcast([N2, DK, HH, N]),
                                  ALU.add).then_inc(st_biased, 1)

            def less_max(b, low, u):
                dve.wait_ge(s_turned, b + 1)
                if low >= 1:
                    dve.wait_ge(sub_done, b)
                s3 = s_ps(u).rearrange("p (g n) -> p g n", n=N)
                dve.tensor_reduce(row_max[:, :], s3, AX.X, ALU.max).then_inc(max_done, 1)
                dve.wait_ge(max_done, b + 1)
                if low >= 2:
                    dve.wait_ge(p_scaled, b - 1)
                dve.tensor_tensor(probs[:, u, :].rearrange("p (g n) -> p g n", n=N), s3,
                                  row_max[:, :].rearrange("p (g o) -> p g o", o=1).to_broadcast([P, 2 * NT, N]),
                                  ALU.subtract).then_inc(sub_done, 1)

            def inverse_sums(b, low, u):
                dve.wait_ge(exp_done, b + 1)
                if low >= 1:
                    dve.wait_ge(inv_done, b)
                dve.tensor_reduce(row_sum[:, :], probs[:, u, :].rearrange("p (g n) -> p g n", n=N), AX.X, ALU.add).then_inc(sum_done, 1)
                dve.wait_ge(sum_done, b + 1)
                if low >= 2:
                    dve.wait_ge(p_scaled, b - 1)
                dve.reciprocal(row_inv[:, u, :], row_sum[:, :]).then_inc(inv_done, 1)

            def own_halves(b, low, u):
                o4 = o_ps(u).rearrange("p (k t n) -> p k t n", k=DK, t=2)
                dve.wait_ge(pv_done, b + 1)
                if low >= 1:
                    dve.wait_ge(o_out, b)
                dve.tensor_scalar(o_part[:, :, :], o4[:, :, 0, :], parity[:, 0:1], None, ALU.mult).then_inc(half_out, 1)
                dve.wait_ge(half_out, b + 1)
                dve.scalar_tensor_tensor(ot[:, :, bass.ds(b * N, N)], o4[:, :, 1, :], parity[:, 1:2], o_part[:, :, :],
                                         ALU.mult, ALU.add).then_inc(o_out, 1)

            def step(s, low, high, u):
                if high < B:
                    add_bias(s, low, u)
                if low >= 1 and high <= B:
                    less_max(s - 1, low - 1, (u + 1) % 2)
                if low >= 2 and high <= B + 1:
                    inverse_sums(s - 2, low - 2, u)
                if low >= 4 and high <= B + 3:
                    own_halves(s - 4, low - 4, u)

            for s in range(6):
                step(s, s, s, s % 2)
            with dve.Fori(6, B - 3, 2) as s:
                for u in range(2):
                    step(s + u, 6, B - 3, u)
            for s in range(B - 2, B + 4):
                step(s, s, s, s % 2)

            for i, (t0, n) in enumerate(TILES):
                dve.wait_ge(o_hi, i + 1)
                dve.tensor_tensor(o_split[1][:, :, t0:t0 + n], ot[:, :, t0:t0 + n], f32(o_split[0][:, :, t0:t0 + n]),
                                  ALU.subtract).then_inc(o_lo, 1)
            for s in range(NT + 2):
                if s < NT:
                    t0, n = TILES[s]
                    dve.wait_ge(wo_done, s + 1)
                    dve.tensor_tensor(h2[0:n, s, :], ps[0:n, s % 4, 0:D], h1[0:n, s, :], ALU.add).then_inc(h2_ready, 1)
                    dve.wait_ge(h2_ready, s + 1)
                    moments(2, s, h2[0:n, s, :])
                if 0 <= s - 1 < NT:
                    i = s - 1
                    turned, seen = (xn_turned, NT - 1 + i) if i < 1 else (x2_turned, i - 1)
                    normed(2, i, TILES[i][1], 2 * NT + i + 1, h2[0:TILES[i][1], i, :], (NT + i) % 2, turned, seen)
                if 0 <= s - 2 < NT:
                    i = s - 2
                    t0, n = TILES[i]
                    dve.wait_ge(x2_hi, i + 1)
                    dve.tensor_tensor(xt[1][:, :, t0:t0 + n],
                                      ps[:, 4 + i % 2, 0:DK * P].rearrange("p (k t) -> p k t", k=DK)[:, :, 0:n],
                                      f32(xt[0][:, :, t0:t0 + n]), ALU.subtract).then_inc(x2_lo, 1)

            chain(dve.memset(gates[:, :, 0:E], 0.0))
            chain(dve.memset(gates[:, :, E:E + TOP], -1.0))
            dve.wait_ge(gate_exp, 1)
            chain(dve.tensor_scalar(gate_e[:, :], gate_e[:, :], 1.0, None, ALU.add))
            dve.reciprocal(gate_t[:, :], gate_e[:, :]).then_inc(gate_sig, 1)
            dve.wait_ge(gate_turned, 1)
            dve.tensor_copy(gates[:, 0:NT - 1, 0:E], ps[:, 4, 0:(NT - 1) * E].rearrange("p (i e) -> p i e", e=E))
            chain(dve.tensor_copy(gates[0:LAST, NT - 1, 0:E], ps[0:LAST, 4, (NT - 1) * E:NT * E]))
            for i in range(NT):
                last = dve.max(top8[:, i, :], gates[:, i, :])
            chain(last)
            chain(dve.memset(top8[:, :, TOP:8], -1.0))
            for i in range(NT):
                last = dve.match_replace(gates_rest[:, i, :], top8[:, i, :], gates[:, i, :], 0.0)
            chain(last)
            dve.tensor_tensor(gates_top[:, :, :], gates[:, :, 0:E], gates_rest[:, :, 0:E], ALU.subtract).then_inc(gate_top, 1)
            dve.wait_ge(gate_back, 1)
            dve.tensor_copy(gate_t[:, :], ps[:, 6:8, :].rearrange("p a n -> p (a n)")[0:E, 0:T]).then_inc(gate_out, 1)

            def apply_gate(e, low, u):
                dve.wait_ge(relu_done, e + 1)
                dve.wait_ge(g_landed[u], 4 * e + (16 - 4 * u))
                if low >= 2:
                    dve.wait_ge(h_lo, e - 1)
                dve.tensor_tensor(hg_f[:, u % 2, :], relu_h[:, u, :], gate_all[:, u, :], ALU.mult).then_inc(gated, 1)

            def low_part(e, u):
                dve.wait_ge(h_hi, e + 1)
                dve.tensor_tensor(hs[1][:, u % 2, :], hg_f[:, u % 2, :], f32(hs[0][:, u % 2, :]), ALU.subtract).then_inc(h_lo, 1)

            apply_gate(0, 0, 0)
            apply_gate(1, 1, 1)
            low_part(0, 0)
            with dve.Fori(RING, E - RING + 1, RING) as e:
                for u in range(RING):
                    apply_gate(e + (u - 2), 2, (u + 2) % RING)
                    low_part(e + (u - 3), (u + 1) % RING)
            for e in range(E - 2, E):
                apply_gate(e, e, e % RING)
                low_part(e - 1, (e - 1) % RING)
            low_part(E - 1, (E - 1) % RING)
            for i, (t0, n) in enumerate(TILES):
                dve.wait_ge(tile_done, min(NT, 2 * (i // 2) + 2))
                if i >= 2:
                    dve.wait_ge(out_stored[i % 2], 16 * (i // 2))
                dve.tensor_tensor(res[0:n, i % 2, :], down_ps(i)[0:n], h2[0:n, i, :], ALU.add).then_inc(res_ready, 1)

        @block.gpsimd
        def _(pool):
            count = [0]

            def chain(ins):
                count[0] += 1
                ins.then_inc(pool_step, 1)
                pool.wait_ge(pool_step, count[0])

            chain(pool.memset(ident[:, :], 0.0))
            pool.affine_select(out=ident[:, :], in_=ident[:, :], compare_op=ALU.not_equal, fill=1.0, base=0,
                               pattern=[[-1, P]], channel_multiplier=1).then_inc(const_done, 2)
            chain(pool.memset(pick[:, :, :], 0.0))
            pool.affine_select(out=pick[:, :, :], in_=pick[:, :, :], compare_op=ALU.not_equal, fill=1.0, base=0,
                               pattern=[[0, B], [-1, N]], channel_multiplier=1).then_inc(const_done, 1)
            chain(pool.memset(head_mask[:, :], 1.0))
            chain(pool.affine_select(out=head_mask[:, :], in_=head_mask[:, :], compare_op=ALU.is_ge, fill=0.0, base=0,
                                     pattern=[[-HD, HH]], channel_multiplier=1))
            pool.affine_select(out=head_mask[:, :], in_=head_mask[:, :], compare_op=ALU.is_ge, fill=0.0, base=HD - 1,
                               pattern=[[HD, HH]], channel_multiplier=-1).then_inc(const_done, 1)
            pool.iota(dist_i[:, :], pattern=[[1, N]], base=0, channel_multiplier=-1).then_inc(const_done, 1)
            pool.memset(neg_half[:, :], -0.5).then_inc(const_done, 1)

            def split(parts, raw, done):
                chain(pool.tensor_copy(parts[0], raw))
                pool.tensor_tensor(parts[1], raw, f32(parts[0]), ALU.subtract).then_inc(done, 1)

            pool.wait_ge(wqk_landed, 48)
            split([a[:, :, Q:KL + 1, :] for a in w], w_raw[:, :, Q:KL + 1, :], w_split)
            pool.wait_ge(wv_landed, 32)
            split([a[:, :, VS:VL + 1, :] for a in w], w_raw[:, :, VS:VL + 1, :], w_split)
            pool.wait_ge(bias_ready, 1)
            pool.affine_select(out=bias_t[:, :], in_=dist[:, 1, :], compare_op=ALU.is_ge, fill=0.0, base=N - 1,
                               pattern=[[0, N]], channel_multiplier=-1).then_inc(const_done, 1)

            def inverse_std(which, i, n, seen):
                pool.wait_ge(var_ready, seen)
                chain(pool.tensor_scalar(veps[0:n, which, i:i + 1], mv[0:n, which, i, 1:2], EPS, None, ALU.add))
                pool.tensor_tensor(rstd[0:n, which, i:i + 1], veps[0:n, which, i:i + 1], neg_half[0:n, :],
                                   ALU.pow).then_inc(rstd_ready, 1)

            seen = 0
            for s in range(NT + 1):
                for which, i in ((0, s), (1, s - 1)):
                    if 0 <= i < NT:
                        seen += 1
                        inverse_std(which, i, TILES[i][1], seen)

            def rest_of_keys(e, u):
                pool.wait_ge(ek_hi, e + 1)
                pool.tensor_tensor(ek[1][:, u], raw_k[:, u, :].rearrange("p (k f) -> p k f", k=DK), f32(ek[0][:, u]),
                                   ALU.subtract).then_inc(k_split, 1)

            def rest_of_values(e, u):
                pool.wait_ge(ev_hi, e + 1)
                pool.tensor_tensor(ev[1][:, u], raw_v[:, u], f32(ev[0][:, u]), ALU.subtract).then_inc(v_split, 1)

            for e in range(RING):
                rest_of_keys(e, e)
                rest_of_values(e, e)
            pool.wait_ge(wo_landed, 16)
            split([a[:, :, WO, :] for a in w], w_raw[:, :, WO, :], w_split)
            pool.wait_ge(q_out, 2)

            def mask_queries(b, low, u):
                if low >= 2:
                    pool.wait_ge(st_done, b - 1)
                q3 = qt[:, :, bass.ds(b * N, N)].rearrange("p k (o n) -> p k o n", o=1).to_broadcast([P, DK, HH, N])
                m3 = head_mask[:, :].rearrange("p (a h o) -> p a h o", a=1, o=1).to_broadcast([P, DK, HH, N])
                pool.tensor_tensor(q_now[:, u].rearrange("p k (h n) -> p k h n", n=N), q3, m3, ALU.mult).then_inc(q_masked, 1)

            def scale_probs(b, low, u):
                pool.wait_ge(inv_done, b + 1)
                if low >= 2:
                    pool.wait_ge(p_turned, b - 1)
                pool.tensor_tensor(probs_n[:, u, :].rearrange("p (g n) -> p g n", n=N),
                                   probs[:, u, :].rearrange("p (g n) -> p g n", n=N),
                                   row_inv[:, u, :].rearrange("p (g o) -> p g o", o=1).to_broadcast([P, 2 * NT, N]),
                                   ALU.mult).then_inc(p_scaled, 1)

            def step(s, low, high, u):
                if high + 1 < B:
                    mask_queries(s + 1, low + 1, (u + 1) % 2)
                if low >= 2 and high <= B + 1:
                    scale_probs(s - 2, low - 2, u)

            mask_queries(0, 0, 0)
            for s in range(6):
                step(s, s, s, s % 2)
            with pool.Fori(6, B - 3, 2) as s:
                for u in range(2):
                    step(s + u, 6, B - 3, u)
            for s in range(B - 2, B + 2):
                step(s, s, s, s % 2)

            for i, (t0, n) in enumerate(TILES):
                inverse_std(2, i, n, 2 * NT + i + 1)
            rest_of_keys(RING, 0)
            rest_of_keys(RING + 1, 1)
            with pool.Fori(RING, E - 2 * RING + 1, RING) as e:
                for u in range(RING):
                    rest_of_keys(e + (u + 2), (u + 2) % RING)
                    rest_of_values(e + u, u)
            for e in range(E - RING, E):
                if e + 2 < E:
                    rest_of_keys(e + 2, (e + 2) % RING)
                rest_of_values(e, e % RING)


_INS = ['x', 'L0_tok_W', 'L0_tok_b', 'L0_tok_cls_token', 'L0_tok_pos_embedding', 'L0_tok_gamma', 'L0_tok_beta',
        'L0_attn_Wq', 'L0_attn_Wkv_short', 'L0_attn_Wkv_long', 'L0_attn_Wo', 'L0_attn_mix_weight',
        'L0_attn_decay_factor', 'L0_ffn_expert_sel', 'L0_ffn_keys', 'L0_ffn_values']


def kernel(**inputs):
    import numpy as _np
    import concourse.bacc as _bacc
    from concourse import mybir as _mybir
    from concourse.bass_utils import run_bass_kernel_spmd as _run

    nc = _bacc.Bacc("TRN2", target_bir_lowering=False, num_devices=1)
    arrays, args = {}, []
    for name in _INS:
        a = _np.ascontiguousarray(inputs[name])
        arrays[f"in_{name}_dram"] = a
        args.append(nc.dram_tensor(f"in_{name}_dram", a.shape, _mybir.dt.from_np(a.dtype), kind="ExternalInput").ap())
    batch, _, side, _ = inputs["x"].shape
    rows = inputs["L0_tok_pos_embedding"].shape[1]
    width = inputs["L0_tok_W"].shape[1]
    out = nc.dram_tensor("out_dram", (batch * rows, width), _mybir.dt.from_np(_np.dtype("float32")), kind="ExternalOutput").ap()
    vit_tower(nc, *args, out)
    r = _run(nc, [arrays], core_ids=[0])
    return r.results[0]["out_dram"].reshape(batch, rows, width)
```

```python
from contextlib import ExitStack

import concourse.bass as bass
from concourse import mybir

F32 = mybir.dt.float32
F32R = mybir.dt.float32r
BF16 = mybir.dt.bfloat16
ALU = mybir.AluOpType
ACT = mybir.ActivationFunctionType
AX = mybir.AxisListType

P = 128
EPS = 1e-5
HEADS = 16
TOP = 4
Q, KS, VS, KL, VL, WO = range(6)


def vit_tower(nc, x, tok_w, tok_b, cls_token, pos, gamma, beta, wq, wkv_short, wkv_long, wo,
              mix_weight, decay_factor, expert_sel, keys, values, out):
    B, C, IMG, _ = x.shape
    PATCH = 16
    G = IMG // PATCH
    N = G * G + 1
    T = B * N
    D = tok_w.shape[1]
    DK = D // P
    KT = tok_w.shape[0] // P
    BH = B * G
    E, _, F = keys.shape
    HD = D // HEADS
    HH = P // HD
    HQ = HH * N
    HALF = T // 2
    BHALF = B // 2
    N2 = 2 * N
    TILES = [(t, min(P, T - t)) for t in range(0, T, P)]
    NT = len(TILES)
    LAST = TILES[-1][1]
    RING = 4
    AHEAD = 8
    assert F == P and HQ == HALF and C * 2 == KT and T % 2 == 0 and HALF % 2 == 0

    with ExitStack() as ctx:
        def sb(name, shape, dt=F32, to=ctx):
            return to.enter_context(nc.sbuf_tensor(name, shape, dt))

        def sem(name):
            return ctx.enter_context(nc.semaphore(name))

        ident = sb("ident", [P, P])
        zeros = sb("zeros", [P, 512], BF16)
        head_mask = sb("head_mask", [P, HH])
        parity = sb("parity", [P, 2])
        neg_half = sb("neg_half", [P, 1])
        bias_t = sb("bias_t", [N2, N])
        dist_i = sb("dist_i", [N2, N], mybir.dt.int32)
        dist = sb("dist", [N2, 2, N])
        scal = sb("scal", [P, 8])
        gam = sb("gam", [P, D])
        bet = sb("bet", [P, D])
        sel_t = [sb(f"sel_t_{p}", [P, DK, P], F32R) for p in ("hi", "lo")]
        h1 = sb("h1", [P, NT, D])
        xn = sb("xn", [P, 2, D])
        stats = sb("stats", [P, 6])
        mv = sb("mv", [P, 3, NT, 2])
        veps = sb("veps", [P, 3, NT])
        rstd = sb("rstd", [P, 3, NT])
        xt = [sb(f"xt_{p}", [P, DK, T], F32R) for p in ("hi", "lo")]
        w_raw = sb("w_raw", [P, DK, 6, D])
        w = [sb(f"w_{p}", [P, DK, 6, D], F32R) for p in ("hi", "lo")]
        raw_k = sb("raw_k", [P, RING, D])
        raw_v = sb("raw_v", [P, RING, D])
        ek = [sb(f"ek_{p}", [P, RING, DK, P], F32R) for p in ("hi", "lo")]
        ev = [sb(f"ev_{p}", [P, RING, D], F32R) for p in ("hi", "lo")]
        early = ExitStack()
        x_in = sb("x_in", [BH, C, PATCH * IMG], to=early)
        x_cols = sb("x_cols", [BH, C, G, PATCH * PATCH], to=early)
        pt = [sb(f"patch_t_{p}", [P, KT, T], F32R, to=early) for p in ("hi", "lo")]
        wt_raw = sb("wt_raw", [P, KT, D], to=early)
        wt = [sb(f"wt_{p}", [P, KT, D], F32R, to=early) for p in ("hi", "lo")]
        pick = sb("pick", [N, B, N], F32R, to=early)
        pos_b = sb("pos_b", [N, D], to=early)
        pos_split = [sb(f"pos_{p}", [N, D], F32R, to=early) for p in ("hi", "lo")]
        first_rows = sb("first_rows", [N, D], to=early)
        bias_rows = sb("bias_rows", [N, D], to=early)
        sel_raw = sb("sel_raw", [E, D], to=early)
        hg = sb("hg", [P, D], to=early)
        early.close()
        qt = sb("qt", [P, DK, T])
        kt = sb("kt", [P, DK, B, 2, N])
        v_sb = sb("v_sb", [P, 2, 2, D])
        k_now = sb("k_now", [P, 2, DK, N2])
        q_now = sb("q_now", [P, 2, DK, HQ])
        st_sb = sb("st_sb", [N2, 2, HEADS * N])
        probs = sb("probs", [P, 2, NT * N2])
        probs_n = sb("probs_n", [P, 2, NT * N2])
        row_max = sb("row_max", [P, 2 * NT])
        row_sum = sb("row_sum", [P, 2 * NT])
        row_inv = sb("row_inv", [P, 2, 2 * NT])
        pt_sb = sb("pt_sb", [N2, 2, HEADS * N])
        v_now = sb("v_now", [N2, 2, D])
        o_part = sb("o_part", [P, DK, N])
        ot = sb("ot", [P, DK, T])
        o_split = [sb(f"o_{p}", [P, DK, T], F32R) for p in ("hi", "lo")]
        h2 = sb("h2", [P, NT, D])
        gate_e = sb("gate_e", [E, T])
        gate_t = sb("gate_t", [E, T])
        gate_x = sb("gate_x", [P, NT, E])
        gates = sb("gates", [P, NT, E + TOP])
        gates_rest = sb("gates_rest", [P, NT, E + TOP])
        gates_top = sb("gates_top", [P, NT, E])
        top8 = sb("top8", [P, NT, 8])
        gate_all = sb("gate_all", [P, RING, T])
        relu_h = sb("relu_h", [P, AHEAD, T])
        hg_f = sb("hg_f", [P, 2, T])
        hs = [sb(f"hs_{p}", [P, 2, T], F32R) for p in ("hi", "lo")]

        ps = ctx.enter_context(nc.psum_tensor("ps", [P, 8, 512], F32))
        v_dram = nc.dram_tensor("v_rows", [T, 2, D], F32, kind="Internal").ap()
        g_dram = nc.dram_tensor("gate_rows", [E, T], F32, kind="Internal").ap()

        x_landed = [sem(f"x_landed{c}") for c in range(C)]
        wt_landed = sem("wt_landed")
        pos_landed, cls_landed, bias_landed, gb_landed, sel_landed, scal_landed = (
            sem(s) for s in ("pos_landed", "cls_landed", "bias_landed", "gb_landed", "sel_landed", "scal_landed"))
        w_landed = [sem(f"w_landed{n}") for n in range(4)]
        k_landed = [sem(f"k_landed{i}") for i in range(RING)]
        v_landed = [sem(f"v_landed{i}") for i in range(RING)]
        g_landed = [sem(f"g_landed{i}") for i in range(RING)]
        x_sorted2 = sem("x_sorted2")
        x_sorted, zeros_done = sem("x_sorted"), sem("zeros_done")
        const_done = sem("const_done")
        pool_step = sem("pool_step")
        dve_step = sem("dve_step")
        wt_hi, wt_lo = sem("wt_hi"), sem("wt_lo")
        sel_turned, sel_hi, sel_lo = sem("sel_turned"), sem("sel_hi"), sem("sel_lo")
        patch_turned, patch_hi, patch_lo = sem("patch_turned"), sem("patch_hi"), sem("patch_lo")
        pos_ready = sem("pos_ready")
        bias_ready, mix_exp, mix_ready, parity_ready = sem("bias_ready"), sem("mix_exp"), sem("mix_ready"), sem("parity_ready")
        tok_done = sem("tok_done")
        h1_ready, logit_out, logit_turned = sem("h1_ready"), sem("logit_out"), sem("logit_turned")
        var_ready, rstd_ready = sem("var_ready"), sem("rstd_ready")
        xn_ready, xn_turned, xt_hi, xt_lo = sem("xn_ready"), sem("xn_turned"), sem("xt_hi"), sem("xt_lo")
        w_hi, w_split = sem("w_hi"), sem("w_split")
        qk_done, qk_out_act, qk_out_dve = sem("qk_done"), sem("qk_out_act"), sem("qk_out_dve")
        v_done, v_out = sem("v_done"), [sem("v_out0"), sem("v_out1")]
        v_stored = [sem("v_stored0"), sem("v_stored1")]
        v_loaded = [sem("v_loaded0"), sem("v_loaded1")]
        k_copied, q_masked = sem("k_copied"), sem("q_masked")
        st_done, st_biased, s_turned = sem("st_done"), sem("st_biased"), sem("s_turned")
        max_done, sub_done, exp_done, sum_done, inv_done = (
            sem(s) for s in ("max_done", "sub_done", "exp_done", "sum_done", "inv_done"))
        p_scaled, p_turned, p_copied, pv_done, half_out, o_out = (
            sem(s) for s in ("p_scaled", "p_turned", "p_copied", "pv_done", "half_out", "o_out"))
        s_cleared = sem("s_cleared")
        o_hi, o_lo, wo_done = sem("o_hi"), sem("o_lo"), sem("wo_done")
        h2_ready, x2_turned, x2_hi, x2_lo = sem("h2_ready"), sem("x2_turned"), sem("x2_hi"), sem("x2_lo")
        logit_done, gate_exp, gate_top, gate_back, gate_out, gate_stored = (
            sem(s) for s in ("logit_done", "gate_exp", "gate_top", "gate_back",
                             "gate_out", "gate_stored"))
        k_split, v_split = sem("k_split"), sem("v_split")
        ek_hi, ev_hi = sem("ek_hi"), sem("ev_hi")
        up_done, relu_done, gated, h_hi, h_lo, down_done = (
            sem(s) for s in ("up_done", "relu_done", "gated", "h_hi", "h_lo", "down_done"))
        tile_done, res_ready = sem("tile_done"), sem("res_ready")
        out_stored = sem("out_stored")

        def f32(ap):
            return ap.bitcast(F32)

        WG = G // 2

        def patch_view(t, k, g):
            v = t[:, k, :].rearrange("p (b n) -> p b n", n=N)[:, :, 1:N]
            return v.rearrange("p b (h w) -> p w b h", w=G)[:, WG * g:WG * g + WG]

        def patch_psum(bank):
            return ps[:, bank, 0:WG * BH].rearrange("p (w b h) -> p w b h", w=WG, b=B)

        st_ps = ps[0:N2, 0:2, 0:HQ]
        pt_ps = ps[:, 4:6, :].rearrange("p a n -> p (a n)")[0:N2, 0:HEADS * N]

        def sorted_x(c):
            return x_cols[:, c].rearrange("p w (r q) -> p w r q", q=PATCH)

        def unsorted_x(c):
            return x_in[:, c, :].rearrange("p (r w q) -> p w r q", r=PATCH, w=G)

        def turned_ps(bank, n):
            return ps[:, bank, 0:DK * P].rearrange("p (k t) -> p k t", k=DK)[:, :, 0:n]

        def images_of(i):
            return min(B, -(-(TILES[i][0] + TILES[i][1]) // N))

        def qk_from_psum(eng, c, j):
            kind, h = j // DK, j % DK
            eng.wait_ge(qk_done, 3 * DK * c + j + 1)
            src = ps[:, 2 + j, 0:HALF]
            if kind == 0:
                nc.scalar.activation(qt[:, h, c * HALF:(c + 1) * HALF], src, ACT.Copy,
                                     scale=float(HD) ** -0.5).then_inc(qk_out_act, 1)
                return
            dst = kt[:, h, c * BHALF:(c + 1) * BHALF, kind - 1, :]
            src = src.rearrange("p (b n) -> p b n", n=N)
            if c == 0:
                nc.scalar.activation(dst, src, ACT.Copy).then_inc(qk_out_act, 1)
            else:
                nc.vector.tensor_copy(dst, src).then_inc(qk_out_dve, 1)

        def s_ps(slot):
            return ps[:, 2 + slot, 0:NT * N2]

        def o_ps(slot):
            return ps[:, 6 + slot, 0:DK * N2]

        def down_ps(i):
            return ps[:, 4 + i // 2, (i % 2) * D:(i % 2) * D + D]

        FIRST_HALF_TILES = -(-HALF // P)
        WARM_UP = 8
        O_SPLIT_AT = {B - 2: (0,), B - 1: (1,), B: (2,), B + 3: (3,)}
        PROJECT_AT = {B: (0, 1), B + 1: (2,), B + 3: (3,)}
        NORM_AT = {B + 1: (0, 1), B + 2: (2,), B + 4: (3,)}
        X_TURN_AT = {B + 2: (0, 1), B + 3: (2,)}
        PROJECT_BANK = (0, 1, 0, 5, 4)

        block = ctx.enter_context(nc.Block())

        @block.sync
        def _(sp):
            for c in range(C):
                x_c = bass.AP(x.tensor, x.offset + c * IMG * IMG,
                              [[C * IMG * IMG, B], [PATCH * IMG, G], [1, PATCH * IMG]])
                sp.dma_start(x_in[:, c, :], x_c).then_inc(x_landed[c], 16)
            for n, (first, count, src) in enumerate(((Q, 1, wq), (KS, 2, wkv_short), (KL, 2, wkv_long), (WO, 1, wo))):
                sp.dma_start(w_raw[:, :, first:first + count, :].rearrange("p k a n -> p k (a n)"),
                             src.rearrange("(k p) n -> p k n", p=P)).then_inc(w_landed[n], 16)

            for vector, dst in ((gamma, gam), (beta, bet)):
                sp.dma_start(dst[:, :], vector.rearrange("(o d) -> o d", o=1).to_broadcast([P, D])).then_inc(gb_landed, 16)
            sp.dma_start(sel_raw[:, :], expert_sel).then_inc(sel_landed, 16)
            for n, one in enumerate((mix_weight, decay_factor)):
                sp.dma_start(scal[:, n:n + 1], one.rearrange("(o d) -> o d", o=1).to_broadcast([P, 1])).then_inc(scal_landed, 16)

            def load_keys(e, slot):
                sp.dma_start(raw_k[:, slot, :].rearrange("p (k f) -> p k f", k=DK),
                             keys[bass.ds(e, 1)].rearrange("o (k p) f -> p (o k) f", p=P)).then_inc(k_landed[slot], 16)

            def load_values(e, slot):
                sp.dma_start(raw_v[:, slot, :],
                             values[bass.ds(e, 1)].rearrange("o p n -> p (o n)")).then_inc(v_landed[slot], 16)

            for e in range(RING):
                load_keys(e, e)
                load_values(e, e)
            for e in range(RING, 2 * RING):
                sp.wait_ge(k_split, e - RING + 1)
                load_keys(e, e - RING)
                sp.wait_ge(v_split, e - RING + 1)
                load_values(e, e - RING)

            for i, (t0, n) in enumerate(TILES):
                sp.wait_ge(v_out[i % 2], i // 2 + 1)
                sp.dma_start(v_dram[t0:t0 + n], v_sb[0:n, i % 2]).then_inc(v_stored[i % 2], 16)
            sp.wait_ge(v_stored[0], 16 * ((NT + 1) // 2))
            sp.wait_ge(v_stored[1], 16 * (NT // 2))

            def load_v(b, slot):
                for n in range(2):
                    sp.dma_start(v_now[n * N:(n + 1) * N, slot, :],
                                 v_dram[bass.ds(b * N, N), n, :]).then_inc(v_loaded[slot], 16)

            load_v(0, 0)
            load_v(1, 1)
            with sp.Fori(2, B - 1, 2) as b:
                for u in range(2):
                    sp.wait_ge(pv_done, b + u - 1)
                    load_v(b + u, u)

            def more_keys(e, u):
                sp.wait_ge(k_split, e - (RING - 1))
                load_keys(e, u)

            def more_values(e, u):
                sp.wait_ge(v_split, e - (RING - 1))
                load_values(e, u)

            more_keys(AHEAD, 0)
            more_keys(AHEAD + 1, 1)
            sp.wait_ge(gate_out, 1)
            sp.dma_start(g_dram, gate_t[:, :]).then_inc(gate_stored, 16)
            sp.wait_ge(gate_stored, 16)

            def load_gate(e, low, u):
                if low >= RING:
                    sp.wait_ge(gated, e - (RING - 1))
                row = g_dram[bass.ds(e, 1), :]
                sp.dma_start(gate_all[:, u, :], row.to_broadcast([P, T])).then_inc(g_landed[u], 16)

            for e in range(RING):
                load_gate(e, e, e)
            more_keys(AHEAD + 2, 2)
            more_keys(AHEAD + 3, 3)
            with sp.Fori(AHEAD, E - 2 * RING + 1, RING) as e:
                for u in range(RING):
                    load_gate(e + (u - RING), RING, u)
                    more_keys(e + (u + RING), u)
                    more_values(e + u, u)
            for e in range(E - RING, E + RING):
                load_gate(e - RING, e - RING, e % RING)
                if e < E:
                    more_values(e, e % RING)

            for i, (t0, n) in enumerate(TILES):
                sp.wait_ge(res_ready, i + 1)
                sp.dma_start(out[t0:t0 + n, :], h2[0:n, i, :]).then_inc(out_stored, 16)
            sp.wait_ge(out_stored, 16 * NT)

        @block.scalar
        def _(act):
            act.dma_start(pos_b[:, :], pos.rearrange("o n d -> (o n) d")).then_inc(pos_landed, 16)
            act.dma_start(bias_rows[:, :], tok_b.rearrange("(o d) -> o d", o=1).to_broadcast([N, D])).then_inc(bias_landed, 16)
            act.dma_start(first_rows[0:1, :], cls_token.rearrange("o n d -> (o n) d")).then_inc(cls_landed, 16)
            act.dma_start(wt_raw[:, :, :], tok_w.rearrange("(k p) n -> p k n", p=P)).then_inc(wt_landed, 16)

            act.wait_ge(x_landed[1], 16)
            act.activation(sorted_x(1), unsorted_x(1), ACT.Copy).then_inc(x_sorted2, 1)
            for g in range(2 * KT):
                act.wait_ge(patch_turned, g + 1)
                act.activation(patch_view(pt[0], g // 2, g % 2), patch_psum(g % 3), ACT.Copy).then_inc(patch_hi, 1)
                if g % 4 == 3:
                    c = g // 4
                    act.wait_ge(wt_landed, 16)
                    act.activation(wt[0][:, 2 * c:2 * c + 2, :], wt_raw[:, 2 * c:2 * c + 2, :], ACT.Copy).then_inc(wt_hi, 1)
            act.wait_ge(scal_landed, 32)
            act.activation(scal[:, 2:3], scal[:, 0:1], ACT.Exp, scale=-1.0).then_inc(mix_exp, 1)
            for n, landed in ((Q, 0), (KS, 1), (KL, 2), (VS, 1), (VL, 2), (WO, 3)):
                act.wait_ge(w_landed[landed], 16)
                act.activation(w[0][:, :, n, :], w_raw[:, :, n, :], ACT.Copy).then_inc(w_hi, 1)
            act.wait_ge(zeros_done, 1)
            act.wait_ge(sel_turned, 1)
            act.activation(sel_t[0][:, :, 0:E], ps[:, 2, 0:DK * E].rearrange("p (k e) -> p k e", k=DK), ACT.Copy).then_inc(sel_hi, 1)

            def high_keys(e, low, u):
                act.wait_ge(k_landed[u], 4 * e + (16 - 4 * u))
                if low >= RING:
                    act.wait_ge(up_done, e - (RING - 1))
                act.activation(ek[0][:, u], raw_k[:, u, :].rearrange("p (k f) -> p k f", k=DK), ACT.Copy).then_inc(ek_hi, 1)

            def high_values(e, low, u):
                act.wait_ge(v_landed[u], 4 * e + (16 - 4 * u))
                if low >= RING:
                    act.wait_ge(down_done, e - (RING - 1))
                act.activation(ev[0][:, u], raw_v[:, u], ACT.Copy).then_inc(ev_hi, 1)

            for e in range(RING):
                high_keys(e, e, e)
                high_values(e, e, e)
            def turned_high(i, bank, turned, done):
                t0, n = TILES[i]
                act.wait_ge(turned, i + 1)
                act.activation(xt[0][:, :, t0:t0 + n], turned_ps(bank, n), ACT.Copy).then_inc(done, 1)

            for i in range(NT):
                turned_high(i, i % 2, xn_turned, xt_hi)
                if i == FIRST_HALF_TILES - 1:
                    for j in range(3):
                        qk_from_psum(act, 0, j)
            for j in range(3, 3 * DK):
                qk_from_psum(act, 0, j)
            for j in range(DK):
                qk_from_psum(act, 1, j)

            def copy_values(i):
                n = TILES[i][1]
                act.wait_ge(v_done, i + 1)
                if i >= 2:
                    act.wait_ge(v_stored[0], 16 * (i // 2))
                for br in range(2):
                    last = act.activation(v_sb[0:n, 0, br, :], ps[0:n, 6, br * D:(br + 1) * D], ACT.Copy,
                                          scale=scal[0:n, 4 + br:5 + br])
                last.then_inc(v_out[0], 1)

            act.wait_ge(mix_ready, 1)
            act.wait_ge(qk_out_dve, 2 * DK)

            def copy_keys(b, low, slot):
                if low >= 2:
                    act.wait_ge(st_done, b - 1)
                act.activation(k_now[:, slot], kt[:, :, bass.ds(b, 1)].rearrange("p k o n m -> p k (o n m)"),
                               ACT.Copy).then_inc(k_copied, 1)

            def exps(b, slot):
                act.wait_ge(sub_done, b + 1)
                act.activation(probs[:, slot, :], probs[:, slot, :], ACT.Exp).then_inc(exp_done, 1)

            def copy_probs(b, low, slot):
                act.wait_ge(p_turned, b + 1)
                if low >= 2:
                    act.wait_ge(pv_done, b - 1)
                act.activation(pt_sb[:, slot, :], pt_ps, ACT.Copy).then_inc(p_copied, 1)

            def own_half(b, low, u):
                act.wait_ge(pv_done, b + 1)
                if low >= 1:
                    act.wait_ge(o_out, b)
                act.activation(o_part[:, :, :], o_ps(u).rearrange("p (k t n) -> p k t n", k=DK, t=2)[:, :, 0, :],
                               ACT.Copy, scale=parity[:, 0:1]).then_inc(half_out, 1)

            def step(s, low, high, u):
                if high + 1 < B:
                    copy_keys(s + 1, low + 1, (u + 1) % 2)
                if low >= 5 and high <= B + 4:
                    own_half(s - 5, low - 5, (u + 1) % 2)
                if low >= 1 and high <= B:
                    exps(s - 1, (u + 1) % 2)
                if low >= 3 and high <= B + 2:
                    copy_probs(s - 3, low - 3, (u + 1) % 2)

            copy_keys(0, 0, 0)
            for s in range(6):
                step(s, s, s, s % 2)
                if 2 * s < NT:
                    copy_values(2 * s)
            with act.Fori(6, B - 3, 2) as s:
                for u in range(2):
                    step(s + u, 6, B - 3, u)

            def attended_high(i):
                t0, n = TILES[i]
                act.wait_ge(o_out, images_of(i))
                act.activation(o_split[0][:, :, t0:t0 + n], ot[:, :, t0:t0 + n], ACT.Copy).then_inc(o_hi, 1)

            for s in range(B - 2, B + 5):
                step(s, s, s, s % 2)
                for i in O_SPLIT_AT.get(s, ()):
                    attended_high(i)
                for i in X_TURN_AT.get(s, ()):
                    turned_high(i, 2 + i % 2, x2_turned, x2_hi)
            attended_high(NT - 1)
            for i in (NT - 2, NT - 1):
                turned_high(i, 2 + i % 2, x2_turned, x2_hi)
            act.wait_ge(logit_done, 1)
            act.activation(gate_t[:, :].rearrange("p (c t) -> p c t", c=2), ps[0:E, 6:8, 0:HALF], ACT.Copy).then_inc(logit_out, 1)
            act.wait_ge(logit_turned, 1)
            act.activation(gate_x[:, 0:NT - 1, :], ps[:, 4, 0:(NT - 1) * E].rearrange("p (i e) -> p i e", e=E), ACT.Exp, scale=-1.0)
            act.activation(gate_x[0:LAST, NT - 1, :], ps[0:LAST, 4, (NT - 1) * E:NT * E], ACT.Exp, scale=-1.0).then_inc(gate_exp, 1)

            def relu(e, low, u):
                act.wait_ge(up_done, e + 1)
                if low >= AHEAD:
                    act.wait_ge(gated, e - (AHEAD - 1))
                act.activation(relu_h[:, u, :].rearrange("p (c t) -> p c t", c=2),
                               ps[:, 2 * (u % 2):2 * (u % 2) + 2, 0:HALF], ACT.Relu).then_inc(relu_done, 1)

            def high_part(e, low, u):
                act.wait_ge(gated, e + 1)
                if low >= 2:
                    act.wait_ge(down_done, e - 1)
                act.activation(hs[0][:, u, :], hg_f[:, u, :], ACT.Copy).then_inc(h_hi, 1)

            for e in range(AHEAD):
                relu(e, e, e)
                if e >= 2:
                    high_keys(e + 2, e + 2, (e + 2) % RING)
                if e >= 6:
                    high_part(e - 6, e - 6, e % 2)
            with act.Fori(AHEAD, E - 2 * AHEAD + 1, AHEAD) as e:
                for u in range(AHEAD):
                    relu(e + u, AHEAD, u)
                    high_keys(e + (u + 2), RING, (u + 2) % RING)
                    high_part(e + (u - 6), 2, u % 2)
                    high_values(e + (u - RING), RING, u % RING)
            for e in range(E - AHEAD, E + 6):
                if e < E:
                    relu(e, e, e % AHEAD)
                if e + 2 < E:
                    high_keys(e + 2, e + 2, (e + 2) % RING)
                high_part(e - 6, e - 6, e % 2)
                if e - RING < E:
                    high_values(e - RING, e - RING, e % RING)

        @block.tensor
        def _(pe):
            def three(dst, stat, mov, first, last, **kw):
                pe.matmul(dst, stat[0], mov[0], start=first, stop=False, **kw)
                pe.matmul(dst, stat[0], mov[1], start=False, stop=False, **kw)
                return pe.matmul(dst, stat[1], mov[0], start=False, stop=last, **kw)

            pe.wait_ge(zeros_done, 1)
            for _ in range(WARM_UP):
                pe.matmul(ps[:, 7, :], zeros[:, 0:P], zeros[:, :], start=True, stop=True)
            pe.wait_ge(const_done, 2)

            def turn_patches(c):
                if c == 1:
                    pe.wait_ge(x_sorted2, 1)
                else:
                    pe.wait_ge(x_sorted, 1 + c // 2)
                for g in range(4 * c, 4 * c + 4):
                    if g >= 3:
                        pe.wait_ge(patch_lo, g - 2)
                    r0 = P * ((g // 2) % 2)
                    for j in range(WG):
                        mm = pe.transpose(ps[:, g % 3, j * BH:(j + 1) * BH],
                                          x_cols[:, c, WG * (g % 2) + j, r0:r0 + P], ident[0:BH, 0:BH])
                    mm.then_inc(patch_turned, 1)

            def embed(i):
                t0, n = TILES[i]
                for k in range(KT):
                    mm = three(ps[0:n, 3 + i, 0:D], [a[:, k, t0:t0 + n] for a in pt], [a[:, k, :] for a in wt],
                               False, k == KT - 1)
                mm.then_inc(tok_done, 1)

            def turn_rows(i, bank, seen, slot, done):
                n = TILES[i][1]
                pe.wait_ge(xn_ready, seen)
                for k in range(DK):
                    mm = pe.transpose(ps[:, bank, k * P:k * P + n], xn[0:n, slot, k * P:(k + 1) * P], ident[0:n, 0:n])
                mm.then_inc(done, 1)

            def turn_first(i):
                if i >= 2:
                    pe.wait_ge(xt_lo, i - 1)
                turn_rows(i, i % 2, i + 1, i % 2, xn_turned)

            turn_patches(0)
            pe.wait_ge(const_done, 3)
            pe.wait_ge(pos_ready, 1)
            for i, (t0, n) in enumerate(TILES):
                for p in range(2):
                    pe.matmul(ps[0:n, 3 + i, 0:D], pick[:].rearrange("p b n -> p (b n)")[:, t0:t0 + n],
                              pos_split[p][:, :], start=p == 0, stop=False)
            turn_patches(1)
            turn_patches(2)
            pe.wait_ge(wt_lo, C)
            pe.wait_ge(patch_lo, 2 * KT)
            embed(0)
            pe.wait_ge(sel_landed, 16)
            for k in range(DK):
                mm = pe.transpose(ps[:, 2, k * E:(k + 1) * E], sel_raw[:, k * P:(k + 1) * P], ident[0:E, 0:E])
            mm.then_inc(sel_turned, 1)
            for i in range(1, NT - 1):
                embed(i)
            turn_first(0)
            embed(NT - 1)
            for i in range(1, FIRST_HALF_TILES):
                turn_first(i)

            def queries_keys(c, j):
                kind, h = (Q, KS, KL)[j // DK], j % DK
                for k in range(DK):
                    mm = three(ps[:, 2 + j, 0:HALF], [a[:, k, kind, h * P:(h + 1) * P] for a in w],
                               [a[:, k, c * HALF:(c + 1) * HALF] for a in xt], k == 0, k == DK - 1)
                mm.then_inc(qk_done, 1)

            pe.wait_ge(w_split, 3)
            pe.wait_ge(sel_lo, 1)
            pe.wait_ge(xt_lo, FIRST_HALF_TILES)
            for j in range(3 * DK):
                if j >= 1:
                    pe.wait_ge(h1_ready, j)
                queries_keys(0, j)
                if j == 2:
                    for i in range(FIRST_HALF_TILES, NT):
                        turn_first(i)
            pe.wait_ge(xt_lo, NT)
            for j in range(3 * DK):
                pe.wait_ge(qk_out_act, j + 1)
                queries_keys(1, j)

            def values_of(i):
                t0, n = TILES[i]
                if i >= 2:
                    pe.wait_ge(v_out[i % 2], i // 2)
                for k in range(DK):
                    mm = three(ps[0:n, 6 + i % 2, :].rearrange("p (a n) -> p a n", a=2), [a[:, k, t0:t0 + n] for a in xt],
                               [a[:, k, VS:VL + 1:2, :] for a in w], k == 0, k == DK - 1)
                mm.then_inc(v_done, 1)

            pe.wait_ge(qk_out_dve, 2 * DK)
            pe.wait_ge(qk_out_act, 4 * DK)
            pe.wait_ge(s_cleared, 1)
            pe.wait_ge(w_split, 5)

            def scores(b, low, u):
                pe.wait_ge(q_masked, b + 1)
                pe.wait_ge(k_copied, b + 1)
                if low >= 1:
                    pe.wait_ge(st_biased, b)
                for h in range(DK):
                    mm = pe.matmul(st_ps[:, h, :], k_now[:, u, h, :], q_now[:, u, h, :], start=True, stop=True)
                mm.then_inc(st_done, 1)

            def turn_scores(b, low, u):
                pe.wait_ge(st_biased, b + 1)
                if low >= 2:
                    pe.wait_ge(sub_done, b - 1)
                for i, (t0, n) in enumerate(TILES):
                    mm = pe.transpose(s_ps(u)[0:n, i * N2:(i + 1) * N2], st_sb[:, u, t0:t0 + n], ident[0:N2, 0:N2])
                mm.then_inc(s_turned, 1)

            def turn_probs(b, low, u):
                pe.wait_ge(p_scaled, b + 1)
                if low >= 1:
                    pe.wait_ge(p_copied, b)
                for i, (t0, n) in enumerate(TILES):
                    mm = pe.transpose(pt_ps[:, t0:t0 + n], probs_n[0:n, u, i * N2:(i + 1) * N2], ident[0:n, 0:n])
                mm.then_inc(p_turned, 1)

            def weigh_values(b, low, u):
                pe.wait_ge(p_copied, b + 1)
                pe.wait_ge(v_loaded[u], 16 * b + (32 - 16 * u))
                if low >= 2:
                    pe.wait_ge(o_out, b - 1)
                for h in range(DK):
                    for j in range(HH // 2):
                        pair = h * (HH // 2) + j
                        mm = pe.matmul(o_ps(u)[32 * j:32 * j + 32, h * N2:(h + 1) * N2], v_now[:, u, 32 * pair:32 * pair + 32],
                                       pt_sb[:, u, pair * N2:(pair + 1) * N2], start=True, stop=True)
                mm.then_inc(pv_done, 1)

            def step(s, low, high, u):
                if low >= 1 and high <= B:
                    turn_scores(s - 1, low - 1, (u + 1) % 2)
                if high < B:
                    scores(s, low, u)
                if low >= 3 and high <= B + 2:
                    turn_probs(s - 3, low - 3, (u + 1) % 2)
                if low >= 4 and high <= B + 3:
                    weigh_values(s - 4, low - 4, u)

            for s in range(6):
                step(s, s, s, s % 2)
                for i in range(2 * s, min(2 * s + 2, NT)):
                    values_of(i)
            with pe.Fori(6, B - 3, 2) as s:
                for u in range(2):
                    step(s + u, 6, B - 3, u)

            def project(i):
                t0, n = TILES[i]
                pe.wait_ge(o_lo, i + 1)
                if i >= 2:
                    pe.wait_ge(h2_ready, i - 1)
                for k in range(DK):
                    mm = three(ps[0:n, PROJECT_BANK[i], 0:D], [a[:, k, t0:t0 + n] for a in o_split],
                               [a[:, k, WO, :] for a in w], k == 0, k == DK - 1)
                mm.then_inc(wo_done, 1)

            def turn_second(i):
                if i >= 2:
                    pe.wait_ge(x2_lo, i - 1)
                turn_rows(i, 2 + i % 2, NT + i + 1, (NT + i) % 2, x2_turned)

            pe.wait_ge(w_split, 6)
            for s in range(B - 2, B + 5):
                step(s, s, s, s % 2)
                if s == B:
                    pe.wait_ge(st_biased, B)
                    pe.wait_ge(sub_done, B)
                for i in PROJECT_AT.get(s, ()):
                    project(i)
                for i in X_TURN_AT.get(s, ()):
                    turn_second(i)

            def logits(c):
                for k in range(DK):
                    mm = three(ps[:, 6 + c, 0:HALF], [a[:, k, :] for a in sel_t],
                               [a[:, k, c * HALF:(c + 1) * HALF] for a in xt], k == 0, k == DK - 1)
                return mm

            def up_half(u, c):
                for k in range(DK):
                    mm = three(ps[:, 2 * (u % 2) + c, 0:HALF], [a[:, u, k, :] for a in ek],
                               [a[:, k, c * HALF:(c + 1) * HALF] for a in xt], k == 0, k == DK - 1)
                return mm

            def expert_up(e, low, u):
                pe.wait_ge(k_split, e + 1)
                if low >= 2:
                    pe.wait_ge(relu_done, e - 1)
                up_half(u, 0)
                up_half(u, 1).then_inc(up_done, 1)

            pe.wait_ge(x2_lo, FIRST_HALF_TILES)
            pe.wait_ge(o_out, B - 1)
            logits(0)
            pe.wait_ge(k_split, 1)
            up_half(0, 0)
            project(NT - 1)
            turn_second(NT - 2)
            turn_second(NT - 1)
            pe.wait_ge(x2_lo, NT)
            pe.wait_ge(o_out, B)
            logits(1).then_inc(logit_done, 1)
            up_half(0, 1).then_inc(up_done, 1)

            def expert_down(e, u, last):
                pe.wait_ge(h_lo, e + 1)
                pe.wait_ge(v_split, e + 1)
                for i, (t0, n) in enumerate(TILES):
                    mm = three(down_ps(i)[0:n], [a[:, u % 2, t0:t0 + n] for a in hs], [a[:, u, :] for a in ev],
                               False, last, skip_group_check=True)
                    if last:
                        mm.then_inc(tile_done, 1)
                if not last:
                    mm.then_inc(down_done, 1)

            pe.wait_ge(logit_out, 1)
            for i, (t0, n) in enumerate(TILES):
                mm = pe.transpose(ps[0:n, 4, i * E:(i + 1) * E], gate_t[:, t0:t0 + n], ident[0:E, 0:E])
            mm.then_inc(logit_turned, 1)
            for e in range(1, 4):
                expert_up(e, e, e % RING)
            pe.wait_ge(gate_top, 1)
            for i, (t0, n) in enumerate(TILES):
                mm = pe.transpose(ps[:, 6:8, :].rearrange("p a n -> p (a n)")[0:E, t0:t0 + n], gates_top[0:n, i, :], ident[0:n, 0:n])
            mm.then_inc(gate_back, 1)
            for e in range(4, AHEAD):
                expert_up(e, e, e % RING)
            pe.wait_ge(gate_out, 1)
            for i in range((NT + 1) // 2):
                pe.matmul(ps[:, 4 + i, :], zeros[:, 0:P], zeros[:, :], start=True, stop=False, skip_group_check=True)
            with pe.Fori(AHEAD, E - RING + 1, RING) as e:
                for u in range(RING):
                    expert_up(e + u, AHEAD, u)
                    expert_down(e + (u - AHEAD), u, False)
            for e in range(E - AHEAD, E):
                expert_down(e, e % RING, e == E - 1)

        @block.vector
        def _(dve):
            count = [0]

            def chain(ins):
                count[0] += 1
                ins.then_inc(dve_step, 1)
                dve.wait_ge(dve_step, count[0])

            dve.memset(f32(sel_t[0][:]), 0.0)
            dve.memset(f32(sel_t[1][:]), 0.0)
            dve.memset(zeros[:], 0.0)
            for a in pt:
                last = dve.memset(f32(a[:].rearrange("p k (b n) -> p k b n", n=N)[:, :, :, 0]), 0.0)
            last.then_inc(zeros_done, 1)

            dve.wait_ge(x_landed[0], 16)
            dve.tensor_copy(sorted_x(0), unsorted_x(0)).then_inc(x_sorted, 1)
            dve.wait_ge(cls_landed, 16)
            dve.wait_ge(bias_landed, 16)
            dve.wait_ge(pos_landed, 16)
            chain(dve.tensor_copy(bias_rows[0:1, :], first_rows[0:1, :]))
            chain(dve.tensor_tensor(pos_b[:, :], pos_b[:, :], bias_rows[:, :], ALU.add))
            chain(dve.tensor_copy(pos_split[0][:, :], pos_b[:, :]))
            dve.tensor_tensor(pos_split[1][:, :], pos_b[:, :], f32(pos_split[0][:, :]), ALU.subtract).then_inc(pos_ready, 1)
            for g in range(2 * KT):
                if g == KT - 2:
                    dve.wait_ge(x_landed[2], 16)
                    dve.tensor_copy(sorted_x(2), unsorted_x(2)).then_inc(x_sorted, 1)
                dve.wait_ge(patch_hi, g + 1)
                dve.tensor_tensor(patch_view(pt[1], g // 2, g % 2), patch_psum(g % 3),
                                  f32(patch_view(pt[0], g // 2, g % 2)), ALU.subtract).then_inc(patch_lo, 1)
                if g % 4 == 3:
                    c = g // 4
                    dve.wait_ge(wt_hi, c + 1)
                    dve.tensor_tensor(wt[1][:, 2 * c:2 * c + 2, :], wt_raw[:, 2 * c:2 * c + 2, :],
                                      f32(wt[0][:, 2 * c:2 * c + 2, :]), ALU.subtract).then_inc(wt_lo, 1)

            dve.wait_ge(const_done, 6)
            dve.wait_ge(scal_landed, 32)
            chain(dve.tensor_copy(dist[:, 0, :], dist_i[:, :]))
            chain(dve.tensor_scalar(dist[:, 1, :], dist[:, 0, :], -1.0, None, ALU.mult))
            chain(dve.tensor_tensor(dist[:, 0, :], dist[:, 0, :], dist[:, 1, :], ALU.max))
            chain(dve.tensor_scalar(scal[:, 3:4], scal[:, 1:2], -1.0, 1.0, ALU.mult, ALU.add))
            dve.tensor_scalar(dist[:, 1, :], dist[:, 0, :], -1.0, scal[0:N2, 3:4], ALU.mult, ALU.mult).then_inc(bias_ready, 1)
            dve.wait_ge(mix_exp, 1)
            chain(dve.tensor_scalar(scal[:, 6:7], scal[:, 2:3], 1.0, None, ALU.add))
            chain(dve.reciprocal(scal[:, 4:5], scal[:, 6:7]))
            chain(dve.tensor_scalar(scal[:, 5:6], scal[:, 4:5], -1.0, 1.0, ALU.mult, ALU.add))
            dve.tensor_reduce(parity[:, :], head_mask[:, :].rearrange("p (j t) -> p t j", t=2), AX.X, ALU.add).then_inc(mix_ready, 1)
            dve.wait_ge(gb_landed, 32)
            dve.wait_ge(sel_hi, 1)
            dve.tensor_tensor(sel_t[1][:, :, 0:E], ps[:, 2, 0:DK * E].rearrange("p (k e) -> p k e", k=DK),
                              f32(sel_t[0][:, :, 0:E]), ALU.subtract).then_inc(sel_lo, 1)

            made = [0]

            def moments(which, i, src):
                if made[0]:
                    dve.wait_ge(var_ready, made[0])
                made[0] += 1
                chain(dve.bn_stats(stats[0:src.shape[0], :], src))
                dve.bn_aggr(mv[0:src.shape[0], which, i, :], stats[0:src.shape[0], :]).then_inc(var_ready, 1)

            def normed(which, i, n, rstd_seen, src, slot, turned, seen):
                dve.wait_ge(rstd_ready, rstd_seen)
                if seen >= 1:
                    dve.wait_ge(turned, seen)
                dve.tensor_scalar(xn[0:n, slot, :], src, mv[0:n, which, i, 0:1], rstd[0:n, which, i:i + 1],
                                  ALU.subtract, ALU.mult).then_inc(xn_ready, 1)

            def turned_low(i, bank, high, done):
                t0, n = TILES[i]
                dve.wait_ge(high, i + 1)
                dve.tensor_tensor(xt[1][:, :, t0:t0 + n], turned_ps(bank, n), f32(xt[0][:, :, t0:t0 + n]),
                                  ALU.subtract).then_inc(done, 1)

            order = []
            for s in range(NT + 3):
                if s < NT:
                    t0, n = TILES[s]
                    dve.wait_ge(tok_done, s + 1)
                    moments(0, s, ps[0:n, 3 + s, 0:D])
                    order.append((0, s))
                if 0 <= s - 1 < NT:
                    i = s - 1
                    t0, n = TILES[i]
                    dve.wait_ge(rstd_ready, order.index((0, i)) + 1)
                    chain(dve.scalar_tensor_tensor(hg[0:n, :], ps[0:n, 3 + i, 0:D], mv[0:n, 0, i, 0:1], gam[0:n, :],
                                                   ALU.subtract, ALU.mult))
                    dve.scalar_tensor_tensor(h1[0:n, i, :], hg[0:n, :], rstd[0:n, 0, i:i + 1], bet[0:n, :],
                                             ALU.mult, ALU.add).then_inc(h1_ready, 1)
                    dve.wait_ge(h1_ready, i + 1)
                    moments(1, i, h1[0:n, i, :])
                    order.append((1, i))
                if 0 <= s - 2 < NT:
                    i = s - 2
                    normed(1, i, TILES[i][1], order.index((1, i)) + 1, h1[0:TILES[i][1], i, :], i % 2, xn_turned, i - 1)
                if 0 <= s - 3 < NT:
                    turned_low(s - 3, (s - 3) % 2, xt_hi, xt_lo)

            for j in range(DK, 3 * DK):
                qk_from_psum(dve, 1, j)

            def copy_values(i):
                n = TILES[i][1]
                dve.wait_ge(v_done, i + 1)
                if i >= 2:
                    dve.wait_ge(v_stored[1], 16 * (i // 2))
                for br in range(2):
                    last = dve.tensor_scalar(v_sb[0:n, 1, br, :], ps[0:n, 7, br * D:(br + 1) * D],
                                             scal[0:n, 4 + br:5 + br], None, ALU.mult)
                last.then_inc(v_out[1], 1)

            dve.wait_ge(qk_out_act, 4 * DK)
            dve.memset(ps[:, 2:4, (NT - 1) * N2:NT * N2], 0.0).then_inc(s_cleared, 1)
            dve.wait_ge(const_done, 7)

            def add_bias(b, low, u):
                dve.wait_ge(st_done, b + 1)
                if low >= 2:
                    dve.wait_ge(s_turned, b - 1)
                dve.tensor_tensor(st_sb[:, u, :].rearrange("p (c h n) -> p c h n", c=DK, n=N),
                                  st_ps.rearrange("p c (h n) -> p c h n", n=N),
                                  bias_t[:, :].rearrange("p (a o n) -> p a o n", a=1, o=1).to_broadcast([N2, DK, HH, N]),
                                  ALU.add).then_inc(st_biased, 1)

            def image_max(b, low, u):
                dve.wait_ge(s_turned, b + 1)
                if low >= 1:
                    dve.wait_ge(sub_done, b)
                dve.tensor_reduce(row_max[:, :], s_ps(u).rearrange("p (g n) -> p g n", n=N), AX.X, ALU.max).then_inc(max_done, 1)

            def less_max(b, low, u):
                dve.wait_ge(max_done, b + 1)
                if low >= 2:
                    dve.wait_ge(p_scaled, b - 1)
                dve.tensor_tensor(probs[:, u, :].rearrange("p (g n) -> p g n", n=N),
                                  s_ps(u).rearrange("p (g n) -> p g n", n=N),
                                  row_max[:, :].rearrange("p (g o) -> p g o", o=1).to_broadcast([P, 2 * NT, N]),
                                  ALU.subtract).then_inc(sub_done, 1)

            def sums(b, low, u):
                dve.wait_ge(exp_done, b + 1)
                if low >= 1:
                    dve.wait_ge(inv_done, b)
                dve.tensor_reduce(row_sum[:, :], probs[:, u, :].rearrange("p (g n) -> p g n", n=N), AX.X, ALU.add).then_inc(sum_done, 1)

            def inverse(b, low, u):
                dve.wait_ge(sum_done, b + 1)
                if low >= 2:
                    dve.wait_ge(p_scaled, b - 1)
                dve.reciprocal(row_inv[:, u, :], row_sum[:, :]).then_inc(inv_done, 1)

            def own_halves(b, u):
                dve.wait_ge(half_out, b + 1)
                dve.scalar_tensor_tensor(ot[:, :, bass.ds(b * N, N)],
                                         o_ps(u).rearrange("p (k t n) -> p k t n", k=DK, t=2)[:, :, 1, :],
                                         parity[:, 1:2], o_part[:, :, :], ALU.mult, ALU.add).then_inc(o_out, 1)

            def step(s, low, high, u):
                if low >= 2 and high <= B + 1:
                    sums(s - 2, low - 2, u)
                if low >= 1 and high <= B:
                    image_max(s - 1, low - 1, (u + 1) % 2)
                if low >= 2 and high <= B + 1:
                    inverse(s - 2, low - 2, u)
                if low >= 1 and high <= B:
                    less_max(s - 1, low - 1, (u + 1) % 2)
                if high < B:
                    add_bias(s, low, u)
                if low >= 5 and high <= B + 4:
                    own_halves(s - 5, (u + 1) % 2)

            for s in range(6):
                step(s, s, s, s % 2)
                if 2 * s + 1 < NT:
                    copy_values(2 * s + 1)
            with dve.Fori(6, B - 3, 2) as s:
                for u in range(2):
                    step(s + u, 6, B - 3, u)

            def attended_low(i):
                t0, n = TILES[i]
                dve.wait_ge(o_hi, i + 1)
                dve.tensor_tensor(o_split[1][:, :, t0:t0 + n], ot[:, :, t0:t0 + n], f32(o_split[0][:, :, t0:t0 + n]),
                                  ALU.subtract).then_inc(o_lo, 1)

            def add_attended(i):
                n = TILES[i][1]
                dve.wait_ge(wo_done, i + 1)
                dve.tensor_tensor(h2[0:n, i, :], ps[0:n, PROJECT_BANK[i], 0:D], h1[0:n, i, :], ALU.add).then_inc(h2_ready, 1)
                dve.wait_ge(h2_ready, i + 1)
                moments(2, i, h2[0:n, i, :])

            def norm_second(i):
                turned, seen = (xn_turned, NT - 1 + i) if i < 1 else (x2_turned, i - 1)
                normed(2, i, TILES[i][1], 2 * NT + i + 1, h2[0:TILES[i][1], i, :], (NT + i) % 2, turned, seen)

            for s in range(B - 2, B + 5):
                step(s, s, s, s % 2)
                for i in O_SPLIT_AT.get(s, ()):
                    attended_low(i)
                for i in PROJECT_AT.get(s, ()):
                    add_attended(i)
                for i in NORM_AT.get(s, ()):
                    norm_second(i)
                for i in X_TURN_AT.get(s, ()):
                    turned_low(i, 2 + i % 2, x2_hi, x2_lo)
            attended_low(NT - 1)
            dve.memset(gates[:, :, 0:E], 0.0)
            chain(dve.memset(gates[:, :, E:E + TOP], -1.0))
            add_attended(NT - 1)
            turned_low(NT - 2, 2 + (NT - 2) % 2, x2_hi, x2_lo)
            norm_second(NT - 1)
            turned_low(NT - 1, 2 + (NT - 1) % 2, x2_hi, x2_lo)

            dve.wait_ge(gate_exp, 1)
            dve.tensor_scalar(gate_x[:, 0:NT - 1, :], gate_x[:, 0:NT - 1, :], 1.0, None, ALU.add)
            chain(dve.tensor_scalar(gate_x[0:LAST, NT - 1, :], gate_x[0:LAST, NT - 1, :], 1.0, None, ALU.add))
            dve.reciprocal(gates[:, 0:NT - 1, 0:E], gate_x[:, 0:NT - 1, :])
            chain(dve.reciprocal(gates[0:LAST, NT - 1, 0:E], gate_x[0:LAST, NT - 1, :]))
            for i in range(NT):
                last = dve.max(top8[:, i, :], gates[:, i, :])
            chain(last)
            chain(dve.memset(top8[:, :, TOP:8], -1.0))
            for i in range(NT):
                last = dve.match_replace(gates_rest[:, i, :], top8[:, i, :], gates[:, i, :], 0.0)
            chain(last)
            dve.tensor_tensor(gates_top[:, :, :], gates[:, :, 0:E], gates_rest[:, :, 0:E], ALU.subtract).then_inc(gate_top, 1)
            dve.wait_ge(gate_back, 1)
            dve.tensor_copy(gate_t[:, :], ps[:, 6:8, :].rearrange("p a n -> p (a n)")[0:E, 0:T]).then_inc(gate_out, 1)

            def apply_gate(e, low, u):
                dve.wait_ge(relu_done, e + 1)
                dve.wait_ge(g_landed[u % RING], 4 * e + (16 - 4 * (u % RING)))
                if low >= 2:
                    dve.wait_ge(h_lo, e - 1)
                dve.tensor_tensor(hg_f[:, u % 2, :], relu_h[:, u, :], gate_all[:, u % RING, :], ALU.mult).then_inc(gated, 1)

            def low_part(e, u):
                dve.wait_ge(h_hi, e + 1)
                dve.tensor_tensor(hs[1][:, u % 2, :], hg_f[:, u % 2, :], f32(hs[0][:, u % 2, :]), ALU.subtract).then_inc(h_lo, 1)

            apply_gate(0, 0, 0)
            apply_gate(1, 1, 1)
            low_part(0, 0)
            with dve.Fori(AHEAD, E - AHEAD + 1, AHEAD) as e:
                for u in range(AHEAD):
                    apply_gate(e + (u - 6), 2, (u + 2) % AHEAD)
                    low_part(e + (u - 7), (u + 1) % 2)
            for e in range(E, E + 7):
                if e - 6 < E:
                    apply_gate(e - 6, e - 6, (e - 6) % AHEAD)
                low_part(e - 7, (e - 7) % 2)
            for i in range(NT):
                n = TILES[i][1]
                dve.wait_ge(tile_done, min(NT, 2 * (i // 2) + 2))
                dve.tensor_tensor(h2[0:n, i, :], down_ps(i)[0:n], h2[0:n, i, :], ALU.add).then_inc(res_ready, 1)

        @block.gpsimd
        def _(pool):
            count = [0]

            def chain(ins):
                count[0] += 1
                ins.then_inc(pool_step, 1)
                pool.wait_ge(pool_step, count[0])

            chain(pool.memset(ident[:, :], 0.0))
            pool.affine_select(out=ident[:, :], in_=ident[:, :], compare_op=ALU.not_equal, fill=1.0, base=0,
                               pattern=[[-1, P]], channel_multiplier=1).then_inc(const_done, 2)
            chain(pool.memset(f32(pick[:, :, :]), 0.0))
            pool.affine_select(out=pick[:, :, :], in_=f32(pick[:, :, :]), compare_op=ALU.not_equal, fill=1.0, base=0,
                               pattern=[[0, B], [-1, N]], channel_multiplier=1).then_inc(const_done, 1)
            chain(pool.memset(head_mask[:, :], 1.0))
            chain(pool.affine_select(out=head_mask[:, :], in_=head_mask[:, :], compare_op=ALU.is_ge, fill=0.0, base=0,
                                     pattern=[[-HD, HH]], channel_multiplier=1))
            pool.affine_select(out=head_mask[:, :], in_=head_mask[:, :], compare_op=ALU.is_ge, fill=0.0, base=HD - 1,
                               pattern=[[HD, HH]], channel_multiplier=-1).then_inc(const_done, 1)
            pool.iota(dist_i[:, :], pattern=[[1, N]], base=0, channel_multiplier=-1).then_inc(const_done, 1)
            pool.memset(neg_half[:, :], -0.5).then_inc(const_done, 1)

            pool.wait_ge(bias_ready, 1)
            pool.affine_select(out=bias_t[:, :], in_=dist[:, 1, :], compare_op=ALU.is_ge, fill=0.0, base=N - 1,
                               pattern=[[0, N]], channel_multiplier=-1).then_inc(const_done, 1)

            def inverse_std(which, i, n, seen):
                pool.wait_ge(var_ready, seen)
                chain(pool.tensor_scalar(veps[0:n, which, i:i + 1], mv[0:n, which, i, 1:2], EPS, None, ALU.add))
                pool.tensor_tensor(rstd[0:n, which, i:i + 1], veps[0:n, which, i:i + 1], neg_half[0:n, :],
                                   ALU.pow).then_inc(rstd_ready, 1)

            def rest_of_weights(m):
                n = (Q, KS, KL, VS, VL, WO)[m]
                pool.wait_ge(w_hi, m + 1)
                pool.tensor_tensor(w[1][:, :, n, :], w_raw[:, :, n, :], f32(w[0][:, :, n, :]), ALU.subtract).then_inc(w_split, 1)

            seen = 0
            for s in range(NT + 1):
                for which, i in ((0, s), (1, s - 1)):
                    if 0 <= i < NT:
                        seen += 1
                        inverse_std(which, i, TILES[i][1], seen)
                rest_of_weights(s)

            def rest_of_keys(e, u):
                pool.wait_ge(ek_hi, e + 1)
                pool.tensor_tensor(ek[1][:, u], raw_k[:, u, :].rearrange("p (k f) -> p k f", k=DK), f32(ek[0][:, u]),
                                   ALU.subtract).then_inc(k_split, 1)

            def rest_of_values(e, u):
                pool.wait_ge(ev_hi, e + 1)
                pool.tensor_tensor(ev[1][:, u], raw_v[:, u], f32(ev[0][:, u]), ALU.subtract).then_inc(v_split, 1)

            for e in range(RING):
                rest_of_keys(e, e)
                rest_of_values(e, e)
            pool.wait_ge(qk_out_act, 4 * DK)

            def mask_queries(b, low, u):
                if low >= 2:
                    pool.wait_ge(st_done, b - 1)
                q3 = qt[:, :, bass.ds(b * N, N)].rearrange("p k (o n) -> p k o n", o=1).to_broadcast([P, DK, HH, N])
                m3 = head_mask[:, :].rearrange("p (a h o) -> p a h o", a=1, o=1).to_broadcast([P, DK, HH, N])
                pool.tensor_tensor(q_now[:, u].rearrange("p k (h n) -> p k h n", n=N), q3, m3, ALU.mult).then_inc(q_masked, 1)

            def scale_probs(b, low, u):
                pool.wait_ge(inv_done, b + 1)
                if low >= 2:
                    pool.wait_ge(p_turned, b - 1)
                pool.tensor_tensor(probs_n[:, u, :].rearrange("p (g n) -> p g n", n=N),
                                   probs[:, u, :].rearrange("p (g n) -> p g n", n=N),
                                   row_inv[:, u, :].rearrange("p (g o) -> p g o", o=1).to_broadcast([P, 2 * NT, N]),
                                   ALU.mult).then_inc(p_scaled, 1)

            def step(s, low, high, u):
                if low >= 2 and high <= B + 1:
                    scale_probs(s - 2, low - 2, u)
                if high + 2 < B:
                    mask_queries(s + 2, low + 2, u)

            mask_queries(0, 0, 0)
            mask_queries(1, 1, 1)
            for s in range(6):
                step(s, s, s, s % 2)
            with pool.Fori(6, B - 3, 2) as s:
                for u in range(2):
                    step(s + u, 6, B - 3, u)
            for s in range(B - 2, B + 2):
                step(s, s, s, s % 2)

            for i, (t0, n) in enumerate(TILES):
                inverse_std(2, i, n, 2 * NT + i + 1)
            for e in range(RING, AHEAD + 2):
                rest_of_keys(e, e % RING)
            with pool.Fori(AHEAD, E - 2 * RING + 1, RING) as e:
                for u in range(RING):
                    rest_of_keys(e + (u + 2), (u + 2) % RING)
                    rest_of_values(e + (u - RING), u)
            for e in range(E - RING, E + RING):
                if e + 2 < E:
                    rest_of_keys(e + 2, (e + 2) % RING)
                rest_of_values(e - RING, e % RING)


_INS = ['x', 'L0_tok_W', 'L0_tok_b', 'L0_tok_cls_token', 'L0_tok_pos_embedding', 'L0_tok_gamma', 'L0_tok_beta',
        'L0_attn_Wq', 'L0_attn_Wkv_short', 'L0_attn_Wkv_long', 'L0_attn_Wo', 'L0_attn_mix_weight',
        'L0_attn_decay_factor', 'L0_ffn_expert_sel', 'L0_ffn_keys', 'L0_ffn_values']


def kernel(**inputs):
    import numpy as _np
    import concourse.bacc as _bacc
    from concourse import mybir as _mybir
    from concourse.bass_utils import run_bass_kernel_spmd as _run

    nc = _bacc.Bacc("TRN2", target_bir_lowering=False, num_devices=1)
    arrays, args = {}, []
    for name in _INS:
        a = _np.ascontiguousarray(inputs[name])
        arrays[f"in_{name}_dram"] = a
        args.append(nc.dram_tensor(f"in_{name}_dram", a.shape, _mybir.dt.from_np(a.dtype), kind="ExternalInput").ap())
    batch, _, side, _ = inputs["x"].shape
    rows = inputs["L0_tok_pos_embedding"].shape[1]
    width = inputs["L0_tok_W"].shape[1]
    out = nc.dram_tensor("out_dram", (batch * rows, width), _mybir.dt.from_np(_np.dtype("float32")), kind="ExternalOutput").ap()
    vit_tower(nc, *args, out)
    r = _run(nc, [arrays], core_ids=[0])
    return r.results[0]["out_dram"].reshape(batch, rows, width)
```

```python
from contextlib import ExitStack

import concourse.bass as bass
from concourse import mybir

F32 = mybir.dt.float32
F32R = mybir.dt.float32r
BF16 = mybir.dt.bfloat16
ALU = mybir.AluOpType
ACT = mybir.ActivationFunctionType
AX = mybir.AxisListType

P = 128
EPS = 1e-5
HEADS = 16
TOP = 4
Q, KS, VS, KL, VL, WO = range(6)


def vit_tower(nc, x, tok_w, tok_b, cls_token, pos, gamma, beta, wq, wkv_short, wkv_long, wo,
              mix_weight, decay_factor, expert_sel, keys, values, out):
    B, C, IMG, _ = x.shape
    PATCH = 16
    G = IMG // PATCH
    N = G * G + 1
    T = B * N
    D = tok_w.shape[1]
    DK = D // P
    KT = tok_w.shape[0] // P
    BH = B * G
    E, _, F = keys.shape
    HD = D // HEADS
    HH = P // HD
    HQ = HH * N
    HALF = T // 2
    BHALF = B // 2
    N2 = 2 * N
    TILES = [(t, min(P, T - t)) for t in range(0, T, P)]
    NT = len(TILES)
    LAST = TILES[-1][1]
    RING = 4
    AHEAD = 8
    assert HEADS == B and F == P and HQ == HALF and C * 2 == KT and T % 2 == 0 and HALF % 2 == 0

    with ExitStack() as ctx:
        def sb(name, shape, dt=F32, to=ctx):
            return to.enter_context(nc.sbuf_tensor(name, shape, dt))

        def sem(name):
            return ctx.enter_context(nc.semaphore(name))

        ident = sb("ident", [P, P])
        zeros = sb("zeros", [P, 512], BF16)
        head_mask = sb("head_mask", [P, HH])
        parity = sb("parity", [P, 2])
        neg_half = sb("neg_half", [P, 1])
        bias_q = sb("bias_q", [P, NT, N])
        dist_i = sb("dist_i", [N, N], mybir.dt.int32)
        dist = sb("dist", [N, 2, N])
        scal = sb("scal", [P, 8])
        gam = sb("gam", [P, D])
        bet = sb("bet", [P, D])
        sel_t = [sb(f"sel_t_{p}", [P, DK, P], F32R) for p in ("hi", "lo")]
        h1 = sb("h1", [P, NT, D])
        xn = sb("xn", [P, 2, D])
        stats = sb("stats", [P, 6])
        mv = sb("mv", [P, 3, NT, 2])
        veps = sb("veps", [P, 3, NT])
        rstd = sb("rstd", [P, 3, NT])
        xt = [sb(f"xt_{p}", [P, DK, T], F32R) for p in ("hi", "lo")]
        w_raw = sb("w_raw", [P, DK, 6, D])
        w = [sb(f"w_{p}", [P, DK, 6, D], F32R) for p in ("hi", "lo")]
        raw_k = sb("raw_k", [P, RING, D])
        raw_v = sb("raw_v", [P, RING, D])
        ek = [sb(f"ek_{p}", [P, RING, DK, P], F32R) for p in ("hi", "lo")]
        ev = [sb(f"ev_{p}", [P, RING, D], F32R) for p in ("hi", "lo")]
        early = ExitStack()
        x_in = sb("x_in", [BH, C, PATCH * IMG], to=early)
        x_cols = sb("x_cols", [BH, C, G, PATCH * PATCH], to=early)
        pt = [sb(f"patch_t_{p}", [P, KT, T], F32R, to=early) for p in ("hi", "lo")]
        wt_raw = sb("wt_raw", [P, KT, D], to=early)
        wt = [sb(f"wt_{p}", [P, KT, D], F32R, to=early) for p in ("hi", "lo")]
        pick = sb("pick", [N, B, N], F32R, to=early)
        pos_b = sb("pos_b", [N, D], to=early)
        pos_split = [sb(f"pos_{p}", [N, D], F32R, to=early) for p in ("hi", "lo")]
        first_rows = sb("first_rows", [N, D], to=early)
        bias_rows = sb("bias_rows", [N, D], to=early)
        sel_raw = sb("sel_raw", [E, D], to=early)
        hg = sb("hg", [P, D], to=early)
        early.close()
        qt = sb("qt", [P, DK, T])
        kt = sb("kt", [P, DK, B, 2, N])
        v_sb = sb("v_sb", [P, 2, 2, D])
        k_now = sb("k_now", [P, 2, DK, N2])
        q_now = sb("q_now", [P, 2, DK * (HQ + P)])
        probs = sb("probs", [P, 2, NT * N2])
        probs_n = sb("probs_n", [P, 2, NT * N2])
        row_max = sb("row_max", [P, 2 * NT])
        row_sum = sb("row_sum", [P, 2 * NT])
        row_inv = sb("row_inv", [P, 2, 2 * NT])
        pt_sb = sb("pt_sb", [N2, 2, HEADS * N])
        v_now = sb("v_now", [N2, 2, D])
        o_part = sb("o_part", [P, DK, N])
        ot = sb("ot", [P, DK, T])
        o_split = [sb(f"o_{p}", [P, DK, T], F32R) for p in ("hi", "lo")]
        h2 = sb("h2", [P, NT, D])
        gate_t = sb("gate_t", [E, T])
        gate_x = sb("gate_x", [P, NT, E])
        gates = sb("gates", [P, NT, E + TOP])
        gates_rest = sb("gates_rest", [P, NT, E + TOP])
        gates_top = sb("gates_top", [P, NT, E])
        top8 = sb("top8", [P, NT, 8])
        gate_all = sb("gate_all", [P, RING, T])
        relu_h = sb("relu_h", [P, AHEAD, T])
        summed = sb("summed", [P, DK, T])
        hg_f = sb("hg_f", [P, 2, T])
        hs = [sb(f"hs_{p}", [P, RING, T], F32R) for p in ("hi", "lo")]

        ps = ctx.enter_context(nc.psum_tensor("ps", [P, 8, 512], F32))
        v_dram = nc.dram_tensor("v_rows", [T, 2, D], F32, kind="Internal").ap()
        g_dram = nc.dram_tensor("gate_rows", [E, T], F32, kind="Internal").ap()

        x_landed = [sem(f"x_landed{c}") for c in range(C)]
        wt_landed = sem("wt_landed")
        pos_landed, cls_landed, bias_landed, gb_landed, sel_landed, scal_landed = (
            sem(s) for s in ("pos_landed", "cls_landed", "bias_landed", "gb_landed", "sel_landed", "scal_landed"))
        w_landed = [sem(f"w_landed{n}") for n in range(4)]
        k_landed = [sem(f"k_landed{i}") for i in range(RING)]
        v_landed = [sem(f"v_landed{i}") for i in range(RING)]
        g_landed = [sem(f"g_landed{i}") for i in range(RING)]
        x_sorted, zeros_done = sem("x_sorted"), sem("zeros_done")
        const_done = sem("const_done")
        pool_step = sem("pool_step")
        dve_step = sem("dve_step")
        wt_hi, wt_lo_pool, wt_lo_dve = sem("wt_hi"), sem("wt_lo_pool"), sem("wt_lo_dve")
        sel_turned, sel_hi, sel_lo = sem("sel_turned"), sem("sel_hi"), sem("sel_lo")
        patch_turned, patch_hi, patch_lo = sem("patch_turned"), sem("patch_hi"), sem("patch_lo")
        pos_ready = sem("pos_ready")
        bias_ready, mix_exp, mix_ready = sem("bias_ready"), sem("mix_exp"), sem("mix_ready")
        tok_done = sem("tok_done")
        h1_ready, logit_out, logit_turned = sem("h1_ready"), sem("logit_out"), sem("logit_turned")
        var_ready, rstd_ready = sem("var_ready"), sem("rstd_ready")
        xn_ready, xn_turned, xt_hi, xt_lo = sem("xn_ready"), sem("xn_turned"), sem("xt_hi"), sem("xt_lo")
        w_hi, w_lo_dve, w_lo_pool = sem("w_hi"), sem("w_lo_dve"), sem("w_lo_pool")
        qk_done, qk_out = sem("qk_done"), sem("qk_out")
        v_done, v_out = sem("v_done"), [sem("v_out0"), sem("v_out1")]
        v_stored = [sem("v_stored0"), sem("v_stored1")]
        v_loaded = [sem("v_loaded0"), sem("v_loaded1")]
        k_copied, q_masked = sem("k_copied"), sem("q_masked")
        s_done, s_biased = sem("s_done"), sem("s_biased")
        bias_spread, bias_kept = sem("bias_spread"), sem("bias_kept")
        max_done, sub_done, exp_done, sum_done, inv_done = (
            sem(s) for s in ("max_done", "sub_done", "exp_done", "sum_done", "inv_done"))
        p_scaled, p_turned, p_copied, pv_done, half_out, o_out = (
            sem(s) for s in ("p_scaled", "p_turned", "p_copied", "pv_done", "half_out", "o_out"))
        s_cleared = sem("s_cleared")
        o_hi, o_lo, o_lo_last, wo_done = sem("o_hi"), sem("o_lo"), sem("o_lo_last"), sem("wo_done")
        h2_ready, x2_turned, x2_hi, x2_lo = sem("h2_ready"), sem("x2_turned"), sem("x2_hi"), sem("x2_lo")
        logit_done, gate_exp, gate_top, gate_back, gate_out, gate_stored = (
            sem(s) for s in ("logit_done", "gate_exp", "gate_top", "gate_back",
                             "gate_out", "gate_stored"))
        k_split, v_split = sem("k_split"), sem("v_split")
        ek_hi, ev_hi = sem("ek_hi"), sem("ev_hi")
        up_done, relu_done, gated, h_hi, h_lo, down_done = (
            sem(s) for s in ("up_done", "relu_done", "gated", "h_hi", "h_lo", "down_done"))
        experts_summed, sum_kept_act, sum_kept_dve, sum_turned, res_ready = (
            sem(s) for s in ("experts_summed", "sum_kept_act", "sum_kept_dve", "sum_turned", "res_ready"))
        out_stored = sem("out_stored")

        def f32(ap):
            return ap.bitcast(F32)

        WG = G // 2

        def patch_view(t, k, g):
            v = t[:, k, :].rearrange("p (b n) -> p b n", n=N)[:, :, 1:N]
            return v.rearrange("p b (h w) -> p w b h", w=G)[:, WG * g:WG * g + WG]

        def patch_psum(bank):
            return ps[:, bank, 0:WG * BH].rearrange("p (w b h) -> p w b h", w=WG, b=B)

        pt_ps = ps[:, 4:6, :].rearrange("p a n -> p (a n)")[0:N2, 0:HEADS * N]

        def sorted_x(c):
            return x_cols[:, c].rearrange("p w (r q) -> p w r q", q=PATCH)

        def unsorted_x(c):
            return x_in[:, c, :].rearrange("p (r w q) -> p w r q", r=PATCH, w=G)

        def turned_ps(bank, n):
            return ps[:, bank, 0:DK * P].rearrange("p (k t) -> p k t", k=DK)[:, :, 0:n]

        def images_of(i):
            return min(B, -(-(TILES[i][0] + TILES[i][1]) // N))

        def qk_bank(c, j):
            return 2 + j if c == 0 else j % 2

        def low_of_embedding(eng, c, done):
            eng.wait_ge(wt_hi, WT_ORDER.index(c) + 1)
            eng.tensor_tensor(wt[1][:, 2 * c:2 * c + 2, :], wt_raw[:, 2 * c:2 * c + 2, :], f32(wt[0][:, 2 * c:2 * c + 2, :]),
                              ALU.subtract).then_inc(done, 1)

        def low_of_weights(eng, m, done):
            eng.wait_ge(w_hi, m + 1)
            eng.tensor_tensor(w[1][:, :, W_ORDER[m], :], w_raw[:, :, W_ORDER[m], :], f32(w[0][:, :, W_ORDER[m], :]),
                              ALU.subtract).then_inc(done, 1)

        def attended_low(eng, i, done):
            t0, n = TILES[i]
            eng.wait_ge(o_hi, i + 1)
            eng.tensor_tensor(o_split[1][:, :, t0:t0 + n], ot[:, :, t0:t0 + n], f32(o_split[0][:, :, t0:t0 + n]),
                              ALU.subtract).then_inc(done, 1)

        def out_parts():
            for i in range(0, NT - 1, 2):
                yield out[i * P:(i + 2) * P, :].rearrange("(a p) d -> p a d", p=P), h2[:, i:i + 2, :]
            yield out[(NT - 1) * P:, :], h2[0:LAST, NT - 1, :]

        def s_ps(slot):
            return ps[:, 2 + slot, 0:NT * N2]

        def spread_bias(i):
            return ps[:, 1, i * N:(i + 1) * N]

        def sum_turned_ps(i):
            return ps[:, i // 2, (i % 2) * D:(i % 2) * D + D]

        def o_ps(slot):
            return ps[:, 6 + slot, 0:DK * N2]

        def down_ps(k, c):
            return ps[:, 4 + 2 * k + c, 0:HALF]

        FIRST_HALF_TILES = -(-HALF // P)
        WARM_UP = 16
        FILL = (6, 14, 0)
        PATCH_BANKS = 4
        WT_ORDER = (2, 0, 1)
        WT_AT = 8
        TURN_BEHIND = 4
        VALUES_BANK = (1, 6, 7, 6, 7)
        PROJECT_BANK = (0, 1, 0, 5, 4)
        X_TURN_BANK = (2, 3, 2, 5, 4)
        W_ORDER = (Q, KS, KL, VS, VL, WO)
        NORM_ORDER = ((0, 0), (0, 1), (1, 0), (0, 2), (1, 1), (2, 0), (1, 2), (2, 1), (0, 3), (3, 0), (2, 2), (0, 4), (3, 1),
                      (3, 2), (1, 3), (1, 4), (2, 3), (2, 4), (3, 3), (3, 4))
        MOMENTS_ORDER = tuple(m for m in NORM_ORDER if m[0] < 2)
        O_HIGH_AT = {B - 2: 0, B - 1: 1, B: 2, B + 3: 3}
        O_LOW_AT = {B - 2: 0, B - 1: 1}
        PROJECT_AT = {B - 1: 0, B: 1, B + 2: 2}
        NORM_AT = {B + 1: 0, B + 2: 1}

        block = ctx.enter_context(nc.Block())

        @block.sync
        def _(sp):
            for c in range(C):
                x_c = bass.AP(x.tensor, x.offset + c * IMG * IMG,
                              [[C * IMG * IMG, B], [PATCH * IMG, G], [1, PATCH * IMG]])
                sp.dma_start(x_in[:, c, :], x_c).then_inc(x_landed[c], 16)
            for n, one in enumerate((mix_weight, decay_factor)):
                sp.dma_start(scal[:, n:n + 1], one.rearrange("(o d) -> o d", o=1).to_broadcast([P, 1])).then_inc(scal_landed, 16)
            for n, (first, count, src) in enumerate(((Q, 1, wq), (KS, 2, wkv_short), (KL, 2, wkv_long), (WO, 1, wo))):
                sp.dma_start(w_raw[:, :, first:first + count, :].rearrange("p k a n -> p k (a n)"),
                             src.rearrange("(k p) n -> p k n", p=P)).then_inc(w_landed[n], 16)

            for vector, dst in ((gamma, gam), (beta, bet)):
                sp.dma_start(dst[:, :], vector.rearrange("(o d) -> o d", o=1).to_broadcast([P, D])).then_inc(gb_landed, 16)
            sp.dma_start(sel_raw[:, :], expert_sel).then_inc(sel_landed, 16)

            def load_keys(e, slot):
                sp.dma_start(raw_k[:, slot, :].rearrange("p (k f) -> p k f", k=DK),
                             keys[bass.ds(e, 1)].rearrange("o (k p) f -> p (o k) f", p=P)).then_inc(k_landed[slot], 16)

            def load_values(e, slot):
                sp.dma_start(raw_v[:, slot, :],
                             values[bass.ds(e, 1)].rearrange("o p n -> p (o n)")).then_inc(v_landed[slot], 16)

            for e in range(RING):
                load_keys(e, e)
                load_values(e, e)
            for e in range(RING, 2 * RING):
                sp.wait_ge(k_split, e - RING + 1)
                load_keys(e, e - RING)
                sp.wait_ge(v_split, e - RING + 1)
                load_values(e, e - RING)

            def store_values(i):
                t0, n = TILES[i]
                sp.wait_ge(v_out[i % 2], i // 2 + 1)
                sp.dma_start(v_dram[t0:t0 + n], v_sb[0:n, i % 2]).then_inc(v_stored[i % 2], 16)

            def load_v(b, slot):
                for n in range(2):
                    sp.dma_start(v_now[n * N:(n + 1) * N, slot, :],
                                 v_dram[bass.ds(b * N, N), n, :]).then_inc(v_loaded[slot], 16)

            store_values(0)
            store_values(1)
            sp.wait_ge(v_stored[0], 16)
            load_v(0, 0)
            load_v(1, 1)
            for i in range(2, NT):
                store_values(i)
            sp.wait_ge(v_stored[0], 16 * ((NT + 1) // 2))
            sp.wait_ge(v_stored[1], 16 * (NT // 2))
            with sp.Fori(2, B - 1, 2) as b:
                for u in range(2):
                    sp.wait_ge(pv_done, b + u - 1)
                    load_v(b + u, u)

            def more_keys(e, u):
                sp.wait_ge(k_split, e - (RING - 1))
                load_keys(e, u)

            def more_values(e, u):
                sp.wait_ge(v_split, e - (RING - 1))
                load_values(e, u)

            more_keys(AHEAD, 0)
            more_keys(AHEAD + 1, 1)
            sp.wait_ge(gate_out, 1)
            sp.dma_start(g_dram, gate_t[:, :]).then_inc(gate_stored, 16)
            sp.wait_ge(gate_stored, 16)

            def load_gate(e, low, u):
                if low >= RING:
                    sp.wait_ge(gated, e - (RING - 1))
                row = g_dram[bass.ds(e, 1), :]
                sp.dma_start(gate_all[:, u, :], row.to_broadcast([P, T])).then_inc(g_landed[u], 16)

            for e in range(RING):
                load_gate(e, e, e)
            more_keys(AHEAD + 2, 2)
            more_keys(AHEAD + 3, 3)
            with sp.Fori(AHEAD, E - 2 * RING + 1, RING) as e:
                for u in range(RING):
                    load_gate(e + (u - RING), RING, u)
                    more_keys(e + (u + RING), u)
                    more_values(e + u, u)
            for e in range(E - 2 * RING, E - RING - 1):
                load_gate(e, e, e % RING)
            for e in range(E - RING, E):
                load_gate(e - 1, e - 1, (e - 1) % RING)
                more_values(e, e % RING)
            load_gate(E - 1, E - 1, (E - 1) % RING)

            for j, (rows, held) in enumerate(out_parts()):
                sp.wait_ge(res_ready, j + 1)
                sp.dma_start(rows, held).then_inc(out_stored, 16)
            sp.wait_ge(out_stored, 16 * ((NT + 1) // 2))

        @block.scalar
        def _(act):
            def qk_from_psum(c, j):
                kind, h = j // DK, j % DK
                act.wait_ge(qk_done, 3 * DK * c + j + 1)
                src = ps[:, qk_bank(c, j), 0:HALF]
                if kind == 0:
                    act.activation(qt[:, h, c * HALF:(c + 1) * HALF], src, ACT.Copy,
                                   scale=float(HD) ** -0.5).then_inc(qk_out, 1)
                else:
                    act.activation(kt[:, h, c * BHALF:(c + 1) * BHALF, kind - 1, :], src.rearrange("p (b n) -> p b n", n=N),
                                   ACT.Copy).then_inc(qk_out, 1)

            act.dma_start(pos_b[:, :], pos.rearrange("o n d -> (o n) d")).then_inc(pos_landed, 16)
            act.dma_start(bias_rows[:, :], tok_b.rearrange("(o d) -> o d", o=1).to_broadcast([N, D])).then_inc(bias_landed, 16)
            act.dma_start(first_rows[0:1, :], cls_token.rearrange("o n d -> (o n) d")).then_inc(cls_landed, 16)
            act.dma_start(wt_raw[:, :, :], tok_w.rearrange("(k p) n -> p k n", p=P)).then_inc(wt_landed, 16)

            def high_of_embedding(c):
                act.activation(wt[0][:, 2 * c:2 * c + 2, :], wt_raw[:, 2 * c:2 * c + 2, :], ACT.Copy).then_inc(wt_hi, 1)

            for g in range(2 * KT):
                if g == WT_AT:
                    act.wait_ge(wt_landed, 16)
                    high_of_embedding(WT_ORDER[0])
                act.wait_ge(patch_turned, g + 1)
                act.activation(patch_view(pt[0], g // 2, g % 2), patch_psum(g % PATCH_BANKS), ACT.Copy).then_inc(patch_hi, 1)
            for c in WT_ORDER[1:]:
                high_of_embedding(c)
            act.wait_ge(scal_landed, 32)
            act.activation(scal[:, 2:3], scal[:, 0:1], ACT.Exp, scale=-1.0).then_inc(mix_exp, 1)
            for n, landed in zip(W_ORDER, (0, 1, 2, 1, 2, 3)):
                act.wait_ge(w_landed[landed], 16)
                act.activation(w[0][:, :, n, :], w_raw[:, :, n, :], ACT.Copy).then_inc(w_hi, 1)
            act.wait_ge(zeros_done, 1)
            act.wait_ge(sel_turned, 1)
            act.activation(sel_t[0][:, :, 0:E], ps[:, 2, 0:DK * E].rearrange("p (k e) -> p k e", k=DK), ACT.Copy).then_inc(sel_hi, 1)

            def high_keys(e, low, u):
                act.wait_ge(k_landed[u], 4 * e + (16 - 4 * u))
                if low >= RING:
                    act.wait_ge(up_done, e - (RING - 1))
                act.activation(ek[0][:, u], raw_k[:, u, :].rearrange("p (k f) -> p k f", k=DK), ACT.Copy).then_inc(ek_hi, 1)

            def high_values(e, low, u):
                act.wait_ge(v_landed[u], 4 * e + (16 - 4 * u))
                if low >= RING:
                    act.wait_ge(down_done, e - (RING - 1))
                act.activation(ev[0][:, u], raw_v[:, u], ACT.Copy).then_inc(ev_hi, 1)

            for e in range(RING):
                high_keys(e, e, e)
                high_values(e, e, e)
            def turned_high(i, bank, turned, done):
                t0, n = TILES[i]
                act.wait_ge(turned, i + 1)
                act.activation(xt[0][:, :, t0:t0 + n], turned_ps(bank, n), ACT.Copy).then_inc(done, 1)

            def values_from_psum(i):
                n = TILES[i][1]
                act.wait_ge(v_done, i + 1)
                if i >= 2:
                    act.wait_ge(v_stored[i % 2], 16 * (i // 2))
                for br in range(2):
                    last = act.activation(v_sb[0:n, i % 2, br, :], ps[0:n, VALUES_BANK[i], br * D:(br + 1) * D], ACT.Copy,
                                          scale=scal[0:n, 4 + br:5 + br])
                last.then_inc(v_out[i % 2], 1)

            for i in range(NT):
                turned_high(i, i % 2, xn_turned, xt_hi)
                if i == FIRST_HALF_TILES - 1:
                    act.wait_ge(mix_ready, 1)
                    values_from_psum(0)
                    for j in range(TURN_BEHIND + 1):
                        qk_from_psum(0, j)
            for j in range(TURN_BEHIND + 1, 3 * DK):
                qk_from_psum(0, j)

            act.wait_ge(qk_out, 3 * DK)

            def copy_keys(b, low, slot):
                if low >= 2:
                    act.wait_ge(s_done, b - 1)
                act.activation(k_now[:, slot], kt[:, :, bass.ds(b, 1)].rearrange("p k o n m -> p k (o n m)"),
                               ACT.Copy).then_inc(k_copied, 1)

            def exps(b, slot):
                act.wait_ge(sub_done, b + 1)
                act.activation(probs[:, slot, :], probs[:, slot, :], ACT.Exp).then_inc(exp_done, 1)

            def copy_probs(b, low, slot):
                act.wait_ge(p_turned, b + 1)
                if low >= 2:
                    act.wait_ge(pv_done, b - 1)
                act.activation(pt_sb[:, slot, :], pt_ps, ACT.Copy).then_inc(p_copied, 1)

            def own_half(b, low, u):
                act.wait_ge(pv_done, b + 1)
                if low >= 1:
                    act.wait_ge(o_out, b)
                act.activation(o_part[:, :, :], o_ps(u).rearrange("p (k t n) -> p k t n", k=DK, t=2)[:, :, 0, :],
                               ACT.Copy, scale=parity[:, 0:1]).then_inc(half_out, 1)

            def step(s, low, high, u):
                if high + 1 < B:
                    copy_keys(s + 1, low + 1, (u + 1) % 2)
                if low >= 5 and high <= B + 4:
                    own_half(s - 5, low - 5, (u + 1) % 2)
                if low >= 1 and high <= B:
                    exps(s - 1, (u + 1) % 2)
                if low >= 3 and high <= B + 2:
                    copy_probs(s - 3, low - 3, (u + 1) % 2)

            copy_keys(0, 0, 0)
            values_from_psum(1)
            for s in range(8):
                if s + 1 == BHALF:
                    act.wait_ge(qk_out, 2 * 3 * DK)
                step(s, s, s, s % 2)
                if s >= 1 and s + 1 < NT:
                    values_from_psum(s + 1)
                if s < 3 * DK:
                    qk_from_psum(1, s)
            with act.Fori(8, B - 3, 2) as s:
                for u in range(2):
                    step(s + u, 8, B - 3, u)

            def attended_high(i):
                t0, n = TILES[i]
                act.wait_ge(o_out, images_of(i))
                act.activation(o_split[0][:, :, t0:t0 + n], ot[:, :, t0:t0 + n], ACT.Copy).then_inc(o_hi, 1)

            for s in range(B - 2, B + 5):
                step(s, s, s, s % 2)
                if s in O_HIGH_AT:
                    attended_high(O_HIGH_AT[s])
            for i in range(NT):
                if i == 1:
                    attended_high(NT - 1)
                turned_high(i, X_TURN_BANK[i], x2_turned, x2_hi)
            act.wait_ge(logit_done, 1)
            act.activation(gate_t[:, :].rearrange("p (c t) -> p c t", c=2), ps[0:E, 6:8, 0:HALF], ACT.Copy).then_inc(logit_out, 1)
            act.wait_ge(logit_turned, 1)
            act.activation(gate_x[:, 0:NT - 1, :], ps[:, 4, 0:(NT - 1) * E].rearrange("p (i e) -> p i e", e=E), ACT.Exp, scale=-1.0)
            act.activation(gate_x[0:LAST, NT - 1, :], ps[0:LAST, 4, (NT - 1) * E:NT * E], ACT.Exp, scale=-1.0).then_inc(gate_exp, 1)

            def relu(e, low, u):
                act.wait_ge(up_done, e + 1)
                if low >= AHEAD:
                    act.wait_ge(gated, e - (AHEAD - 1))
                act.activation(relu_h[:, u, :].rearrange("p (c t) -> p c t", c=2),
                               ps[:, 2 * (u % 2):2 * (u % 2) + 2, 0:HALF], ACT.Relu).then_inc(relu_done, 1)

            def high_part(e, low, u):
                act.wait_ge(gated, e + 1)
                if low >= RING:
                    act.wait_ge(down_done, e - (RING - 1))
                act.activation(hs[0][:, u, :], hg_f[:, u % 2, :], ACT.Copy).then_inc(h_hi, 1)

            for e in range(AHEAD):
                relu(e, e, e)
                if e >= 1:
                    high_keys(e + 3, e + 3, (e + 3) % RING)
                if e >= 6:
                    high_part(e - 6, e - 6, (e - 6) % RING)
            with act.Fori(AHEAD, E - 2 * AHEAD + 1, AHEAD) as e:
                for u in range(AHEAD):
                    relu(e + u, AHEAD, u)
                    high_keys(e + (u + 3), RING, (u + 3) % RING)
                    high_part(e + (u - 6), 2 if u < 2 else RING, (u + 2) % RING)
                    high_values(e + (u - RING), RING, u % RING)
            for e in range(E - AHEAD, E + 6):
                if e < E:
                    relu(e, e, e % AHEAD)
                if e + 3 < E:
                    high_keys(e + 3, e + 3, (e + 3) % RING)
                high_part(e - 6, e - 6, (e - 6) % RING)
                if e - RING < E:
                    high_values(e - RING, e - RING, e % RING)
            for c in range(2):
                act.wait_ge(experts_summed, c + 1)
                act.activation(summed[:, 0, c * HALF:(c + 1) * HALF], down_ps(0, c), ACT.Copy).then_inc(sum_kept_act, 1)

        @block.tensor
        def _(pe):
            def three(dst, stat, mov, first, last, **kw):
                pe.matmul(dst, stat[0], mov[0], start=first, stop=False, **kw)
                pe.matmul(dst, stat[0], mov[1], start=False, stop=False, **kw)
                return pe.matmul(dst, stat[1], mov[0], start=False, stop=last, **kw)

            def keep_clock(count):
                for _ in range(count):
                    pe.matmul(ps[:, 7, D:2 * D], zeros[:, 0:P], zeros[:, 0:D], start=True, stop=True)

            pe.wait_ge(zeros_done, 1)
            keep_clock(WARM_UP)
            pe.wait_ge(const_done, 2)

            def turn_patches(c):
                pe.wait_ge(x_sorted, c + 1)
                for g in range(4 * c, 4 * c + 4):
                    if g >= PATCH_BANKS:
                        pe.wait_ge(patch_lo, g - (PATCH_BANKS - 1))
                    r0 = P * ((g // 2) % 2)
                    for j in range(WG):
                        mm = pe.transpose(ps[:, g % PATCH_BANKS, j * BH:(j + 1) * BH],
                                          x_cols[:, c, WG * (g % 2) + j, r0:r0 + P], ident[0:BH, 0:BH])
                    mm.then_inc(patch_turned, 1)
                keep_clock(FILL[c])

            def embed(i):
                t0, n = TILES[i]
                for k in range(KT):
                    if i == 0 and k in (0, 2):
                        pe.wait_ge(wt_lo_dve, k // 2 + 1)
                    if i == 0 and k == 4:
                        pe.wait_ge(wt_lo_pool, 1)
                    mm = three(ps[0:n, 3 + i, 0:D], [a[:, k, t0:t0 + n] for a in pt], [a[:, k, :] for a in wt],
                               False, k == KT - 1)
                mm.then_inc(tok_done, 1)

            def turn_rows(i, bank, seen, slot, done):
                n = TILES[i][1]
                pe.wait_ge(xn_ready, seen)
                for k in range(DK):
                    mm = pe.transpose(ps[:, bank, k * P:k * P + n], xn[0:n, slot, k * P:(k + 1) * P], ident[0:n, 0:n])
                mm.then_inc(done, 1)

            def turn_first(i):
                if i == 1:
                    pe.wait_ge(bias_kept, 1)
                if i >= 2:
                    pe.wait_ge(xt_lo, i - 1)
                turn_rows(i, i % 2, i + 1, i % 2, xn_turned)

            def pick_rows(i):
                t0, n = TILES[i]
                for p in range(2):
                    pe.matmul(ps[0:n, 3 + i, 0:D], pick[:].rearrange("p b n -> p (b n)")[:, t0:t0 + n],
                              pos_split[p][:, :], start=p == 0, stop=False)

            turn_patches(0)
            turn_patches(1)
            turn_patches(2)
            pe.wait_ge(const_done, 3)
            pe.wait_ge(pos_ready, 1)
            for i in range(1, NT):
                pick_rows(i)
            pe.wait_ge(patch_lo, 2 * KT)
            pick_rows(0)
            embed(0)
            pe.wait_ge(sel_landed, 16)
            for k in range(DK):
                mm = pe.transpose(ps[:, 2, k * E:(k + 1) * E], sel_raw[:, k * P:(k + 1) * P], ident[0:E, 0:E])
            mm.then_inc(sel_turned, 1)
            pe.wait_ge(bias_ready, 1)
            for i, (t0, n) in enumerate(TILES):
                mm = pe.matmul(spread_bias(i)[0:n], f32(pick[:].rearrange("p b n -> p (b n)")[:, t0:t0 + n]), dist[:, 1, :],
                               start=True, stop=True)
            mm.then_inc(bias_spread, 1)
            for i in range(1, NT):
                embed(i)
            for i in range(FIRST_HALF_TILES):
                turn_first(i)

            def queries_keys(c, j):
                kind, h = (Q, KS, KL)[j // DK], j % DK
                for k in range(DK):
                    mm = three(ps[:, qk_bank(c, j), 0:HALF], [a[:, k, kind, h * P:(h + 1) * P] for a in w],
                               [a[:, k, c * HALF:(c + 1) * HALF] for a in xt], k == 0, k == DK - 1)
                mm.then_inc(qk_done, 1)

            def values_of(i):
                t0, n = TILES[i]
                for k in range(DK):
                    mm = three(ps[0:n, VALUES_BANK[i], :].rearrange("p (a n) -> p a n", a=2), [a[:, k, t0:t0 + n] for a in xt],
                               [a[:, k, VS:VL + 1:2, :] for a in w], k == 0, k == DK - 1)
                mm.then_inc(v_done, 1)

            pe.wait_ge(w_lo_dve, 3)
            pe.wait_ge(w_lo_pool, 2)
            pe.wait_ge(xt_lo, 2)
            values_of(0)
            pe.wait_ge(sel_lo, 1)
            pe.wait_ge(xt_lo, FIRST_HALF_TILES)
            for j in range(3 * DK):
                if j >= 1:
                    pe.wait_ge(h1_ready, j)
                queries_keys(0, j)
                if j == TURN_BEHIND:
                    pe.wait_ge(v_out[0], 1)
                    for i in range(FIRST_HALF_TILES, NT):
                        turn_first(i)
            pe.wait_ge(qk_out, 5)
            values_of(1)

            pe.wait_ge(s_cleared, 1)

            def scores(b, low, u):
                pe.wait_ge(q_masked, b + 1)
                pe.wait_ge(k_copied, b + 1)
                if low >= 2:
                    pe.wait_ge(sub_done, b - 1)
                for i, (t0, n) in enumerate(TILES):
                    halves = [k for k in range(DK) if t0 < (k + 1) * HQ and t0 + n > k * HQ]
                    for k in halves:
                        mm = pe.matmul(s_ps(u)[0:n, i * N2:(i + 1) * N2], q_now[:, u, t0 + k * P:t0 + k * P + n],
                                       k_now[:, u, k, :], start=k == halves[0], stop=k == halves[-1])
                mm.then_inc(s_done, 1)

            def turn_probs(b, low, u):
                pe.wait_ge(p_scaled, b + 1)
                if low >= 1:
                    pe.wait_ge(p_copied, b)
                for i, (t0, n) in enumerate(TILES):
                    mm = pe.transpose(pt_ps[:, t0:t0 + n], probs_n[0:n, u, i * N2:(i + 1) * N2], ident[0:n, 0:n])
                mm.then_inc(p_turned, 1)

            def weigh_values(b, low, u):
                pe.wait_ge(p_copied, b + 1)
                pe.wait_ge(v_loaded[u], 16 * b + (32 - 16 * u))
                if low < 2:
                    pe.wait_ge(v_out[(NT - 2 + low) % 2], (NT + low) // 2)
                if low >= 2:
                    pe.wait_ge(o_out, b - 1)
                for h in range(DK):
                    for j in range(HH // 2):
                        pair = h * (HH // 2) + j
                        mm = pe.matmul(o_ps(u)[32 * j:32 * j + 32, h * N2:(h + 1) * N2], v_now[:, u, 32 * pair:32 * pair + 32],
                                       pt_sb[:, u, pair * N2:(pair + 1) * N2], start=True, stop=True)
                mm.then_inc(pv_done, 1)

            def step(s, low, high, u):
                if high < B:
                    scores(s, low, u)
                if low >= 3 and high <= B + 2:
                    turn_probs(s - 3, low - 3, (u + 1) % 2)
                if low >= 4 and high <= B + 3:
                    weigh_values(s - 4, low - 4, u)

            for s in range(8):
                step(s, s, s, s % 2)
                if s >= 1 and s + 1 < NT:
                    if s == 1:
                        pe.wait_ge(qk_out, 3 * DK)
                    if s >= 2:
                        pe.wait_ge(v_out[(s + 1) % 2], (s - 1) // 2 + 1)
                    values_of(s + 1)
                if s < 3 * DK:
                    if s == 0:
                        pe.wait_ge(xt_lo, NT)
                    if s >= 2:
                        pe.wait_ge(qk_out, 3 * DK + s - 1)
                    queries_keys(1, s)
            with pe.Fori(8, B - 3, 2) as s:
                for u in range(2):
                    step(s + u, 8, B - 3, u)

            def project(i):
                t0, n = TILES[i]
                if i < NT - 1:
                    pe.wait_ge(o_lo, i + 1)
                else:
                    pe.wait_ge(o_lo_last, 1)
                if i >= 2:
                    pe.wait_ge(h2_ready, i - 1)
                for k in range(DK):
                    mm = three(ps[0:n, PROJECT_BANK[i], 0:D], [a[:, k, t0:t0 + n] for a in o_split],
                               [a[:, k, WO, :] for a in w], k == 0, k == DK - 1)
                mm.then_inc(wo_done, 1)

            def turn_second(i):
                if i == 0:
                    pe.wait_ge(sub_done, B)
                if i >= 2:
                    pe.wait_ge(x2_lo, i - 1)
                turn_rows(i, X_TURN_BANK[i], NT + i + 1, (NT + i) % 2, x2_turned)

            pe.wait_ge(w_lo_pool, 3)
            for s in range(B - 2, B + 5):
                step(s, s, s, s % 2)
                if s in PROJECT_AT:
                    project(PROJECT_AT[s])

            def logits(c):
                for k in range(DK):
                    mm = three(ps[:, 6 + c, 0:HALF], [a[:, k, :] for a in sel_t],
                               [a[:, k, c * HALF:(c + 1) * HALF] for a in xt], k == 0, k == DK - 1)
                return mm

            def up_half(u, c):
                for k in range(DK):
                    mm = three(ps[:, 2 * (u % 2) + c, 0:HALF], [a[:, u, k, :] for a in ek],
                               [a[:, k, c * HALF:(c + 1) * HALF] for a in xt], k == 0, k == DK - 1)
                return mm

            def expert_up(e, low, u):
                pe.wait_ge(k_split, e + 1)
                if low >= 2:
                    pe.wait_ge(relu_done, e - 1)
                up_half(u, 0)
                up_half(u, 1).then_inc(up_done, 1)

            turn_second(0)
            turn_second(1)
            project(3)
            turn_second(2)
            project(4)
            pe.wait_ge(x2_lo, FIRST_HALF_TILES)
            pe.wait_ge(o_out, B - 1)
            logits(0)
            turn_second(3)
            pe.wait_ge(k_split, 1)
            up_half(0, 0)
            pe.wait_ge(k_split, 2)
            up_half(1, 0)
            turn_second(4)
            pe.wait_ge(x2_lo, NT)
            pe.wait_ge(o_out, B)
            logits(1).then_inc(logit_done, 1)
            up_half(0, 1).then_inc(up_done, 1)

            def expert_down(e, u, last):
                pe.wait_ge(h_lo, e + 1)
                pe.wait_ge(v_split, e + 1)
                for c in range(2):
                    for k in range(DK):
                        mm = three(down_ps(k, c), [a[:, u, k * P:(k + 1) * P] for a in ev],
                                   [a[:, u, c * HALF:(c + 1) * HALF] for a in hs], False, last, skip_group_check=True)
                    if last:
                        mm.then_inc(experts_summed, 1)
                if not last:
                    mm.then_inc(down_done, 1)

            pe.wait_ge(logit_out, 1)
            for i, (t0, n) in enumerate(TILES):
                mm = pe.transpose(ps[0:n, 4, i * E:(i + 1) * E], gate_t[:, t0:t0 + n], ident[0:E, 0:E])
            mm.then_inc(logit_turned, 1)
            up_half(1, 1).then_inc(up_done, 1)
            for e in range(2, 4):
                expert_up(e, e, e % RING)
            pe.wait_ge(gate_top, 1)
            for i, (t0, n) in enumerate(TILES):
                mm = pe.transpose(ps[:, 6:8, :].rearrange("p a n -> p (a n)")[0:E, t0:t0 + n], gates_top[0:n, i, :], ident[0:n, 0:n])
            mm.then_inc(gate_back, 1)
            for e in range(4, AHEAD):
                expert_up(e, e, e % RING)
            pe.wait_ge(gate_out, 1)
            for k in range(DK):
                for c in range(2):
                    pe.matmul(down_ps(k, c), zeros[:, 0:P], zeros[:, 0:HALF], start=True, stop=False, skip_group_check=True)
            with pe.Fori(AHEAD, E - RING + 1, RING) as e:
                for u in range(RING):
                    expert_up(e + u, AHEAD, u)
                    expert_down(e + (u - AHEAD), u, False)
            for e in range(E - AHEAD, E):
                expert_down(e, e % RING, e == E - 1)
            for i, (t0, n) in enumerate(TILES):
                if i == 0:
                    pe.wait_ge(relu_done, E)
                if i in (0, FIRST_HALF_TILES - 1):
                    pe.wait_ge(sum_kept_act, 1 + min(i, 1))
                    pe.wait_ge(sum_kept_dve, 1 + min(i, 1))
                for k in range(DK):
                    mm = pe.transpose(sum_turned_ps(i)[0:n, k * P:(k + 1) * P], summed[:, k, t0:t0 + n], ident[:, :])
                if i % 2 == 1 or i == NT - 1:
                    mm.then_inc(sum_turned, 1)

        @block.vector
        def _(dve):
            count = [0]

            def chain(ins):
                count[0] += 1
                ins.then_inc(dve_step, 1)
                dve.wait_ge(dve_step, count[0])

            dve.memset(f32(sel_t[0][:]), 0.0)
            dve.memset(f32(sel_t[1][:]), 0.0)
            dve.memset(zeros[:], 0.0)
            dve.memset(bias_q[:, NT - 1, :], 0.0)
            for a in pt:
                last = dve.memset(f32(a[:].rearrange("p k (b n) -> p k b n", n=N)[:, :, :, 0]), 0.0)
            last.then_inc(zeros_done, 1)

            for c in range(2):
                dve.wait_ge(x_landed[c], 16)
                dve.tensor_copy(sorted_x(c), unsorted_x(c)).then_inc(x_sorted, 1)
            for g in range(2 * KT):
                if g == 2 * KT // C:
                    dve.wait_ge(x_landed[2], 16)
                    dve.tensor_copy(sorted_x(2), unsorted_x(2)).then_inc(x_sorted, 1)
                dve.wait_ge(patch_hi, g + 1)
                dve.tensor_tensor(patch_view(pt[1], g // 2, g % 2), patch_psum(g % PATCH_BANKS),
                                  f32(patch_view(pt[0], g // 2, g % 2)), ALU.subtract).then_inc(patch_lo, 1)
            for c in range(2):
                low_of_embedding(dve, c, wt_lo_dve)

            dve.wait_ge(const_done, 6)
            dve.wait_ge(scal_landed, 32)
            chain(dve.tensor_copy(dist[:, 0, :], dist_i[:, :]))
            chain(dve.tensor_scalar(dist[:, 1, :], dist[:, 0, :], -1.0, None, ALU.mult))
            chain(dve.tensor_tensor(dist[:, 0, :], dist[:, 0, :], dist[:, 1, :], ALU.max))
            chain(dve.tensor_scalar(scal[:, 3:4], scal[:, 1:2], -1.0, 1.0, ALU.mult, ALU.add))
            dve.tensor_scalar(dist[:, 1, :], dist[:, 0, :], -1.0, scal[0:N, 3:4], ALU.mult, ALU.mult).then_inc(bias_ready, 1)
            dve.wait_ge(mix_exp, 1)
            chain(dve.tensor_scalar(scal[:, 6:7], scal[:, 2:3], 1.0, None, ALU.add))
            chain(dve.reciprocal(scal[:, 4:5], scal[:, 6:7]))
            chain(dve.tensor_scalar(scal[:, 5:6], scal[:, 4:5], -1.0, 1.0, ALU.mult, ALU.add))
            dve.tensor_reduce(parity[:, :], head_mask[:, :].rearrange("p (j t) -> p t j", t=2), AX.X, ALU.add).then_inc(mix_ready, 1)
            for m in range(0, len(W_ORDER), 2):
                low_of_weights(dve, m, w_lo_dve)

            made = [0]

            def moments(which, i, src):
                if made[0]:
                    dve.wait_ge(var_ready, made[0])
                made[0] += 1
                chain(dve.bn_stats(stats[0:src.shape[0], :], src))
                dve.bn_aggr(mv[0:src.shape[0], which, i, :], stats[0:src.shape[0], :]).then_inc(var_ready, 1)

            def normed(which, i, n, rstd_seen, src, slot, turned, seen):
                dve.wait_ge(rstd_ready, rstd_seen)
                if seen >= 1:
                    dve.wait_ge(turned, seen)
                dve.tensor_scalar(xn[0:n, slot, :], src, mv[0:n, which, i, 0:1], rstd[0:n, which, i:i + 1],
                                  ALU.subtract, ALU.mult).then_inc(xn_ready, 1)

            def turned_low(i, bank, high, done):
                t0, n = TILES[i]
                dve.wait_ge(high, i + 1)
                dve.tensor_tensor(xt[1][:, :, t0:t0 + n], turned_ps(bank, n), f32(xt[0][:, :, t0:t0 + n]),
                                  ALU.subtract).then_inc(done, 1)

            def first_norm(i):
                n = TILES[i][1]
                dve.wait_ge(rstd_ready, MOMENTS_ORDER.index((0, i)) + 1)
                chain(dve.scalar_tensor_tensor(hg[0:n, :], ps[0:n, 3 + i, 0:D], mv[0:n, 0, i, 0:1], gam[0:n, :],
                                               ALU.subtract, ALU.mult))
                dve.scalar_tensor_tensor(h1[0:n, i, :], hg[0:n, :], rstd[0:n, 0, i:i + 1], bet[0:n, :],
                                         ALU.mult, ALU.add).then_inc(h1_ready, 1)
                dve.wait_ge(h1_ready, i + 1)
                moments(1, i, h1[0:n, i, :])

            def keep_selection_and_bias():
                dve.wait_ge(sel_hi, 1)
                dve.tensor_tensor(sel_t[1][:, :, 0:E], ps[:, 2, 0:DK * E].rearrange("p (k e) -> p k e", k=DK),
                                  f32(sel_t[0][:, :, 0:E]), ALU.subtract).then_inc(sel_lo, 1)
                dve.wait_ge(bias_spread, 1)
                dve.tensor_copy(bias_q[:, 0:NT - 1, :], ps[:, 1, 0:(NT - 1) * N].rearrange("p (i n) -> p i n", n=N))
                dve.tensor_copy(bias_q[0:LAST, NT - 1, :], spread_bias(NT - 1)[0:LAST]).then_inc(bias_kept, 1)

            dve.wait_ge(gb_landed, 32)
            for stage, i in NORM_ORDER:
                n = TILES[i][1]
                if stage == 0:
                    dve.wait_ge(tok_done, i + 1)
                    moments(0, i, ps[0:n, 3 + i, 0:D])
                    if i == 0:
                        keep_selection_and_bias()
                elif stage == 1:
                    first_norm(i)
                elif stage == 2:
                    normed(1, i, n, MOMENTS_ORDER.index((1, i)) + 1, h1[0:n, i, :], i % 2, xn_turned, i - 1)
                else:
                    turned_low(i, i % 2, xt_hi, xt_lo)

            dve.wait_ge(qk_out, 2)
            dve.memset(ps[:, 2:4, (NT - 1) * N2:NT * N2], 0.0).then_inc(s_cleared, 1)

            def add_bias(b, u):
                dve.wait_ge(s_done, b + 1)
                near = s_ps(u).rearrange("p (i r n) -> p i r n", i=NT, n=N)[:, :, 0, :]
                dve.tensor_tensor(near, near, bias_q[:, :, :], ALU.add).then_inc(s_biased, 1)

            def image_max(b, low, u):
                dve.wait_ge(s_biased, b + 1)
                if low >= 1:
                    dve.wait_ge(sub_done, b)
                dve.tensor_reduce(row_max[:, :], s_ps(u).rearrange("p (g n) -> p g n", n=N), AX.X, ALU.max).then_inc(max_done, 1)

            def less_max(b, low, u):
                dve.wait_ge(max_done, b + 1)
                if low >= 2:
                    dve.wait_ge(p_scaled, b - 1)
                dve.tensor_tensor(probs[:, u, :].rearrange("p (g n) -> p g n", n=N),
                                  s_ps(u).rearrange("p (g n) -> p g n", n=N),
                                  row_max[:, :].rearrange("p (g o) -> p g o", o=1).to_broadcast([P, 2 * NT, N]),
                                  ALU.subtract).then_inc(sub_done, 1)

            def sums(b, low, u):
                dve.wait_ge(exp_done, b + 1)
                if low >= 1:
                    dve.wait_ge(inv_done, b)
                dve.tensor_reduce(row_sum[:, :], probs[:, u, :].rearrange("p (g n) -> p g n", n=N), AX.X, ALU.add).then_inc(sum_done, 1)

            def inverse(b, low, u):
                dve.wait_ge(sum_done, b + 1)
                if low >= 2:
                    dve.wait_ge(p_scaled, b - 1)
                dve.reciprocal(row_inv[:, u, :], row_sum[:, :]).then_inc(inv_done, 1)

            def own_halves(b, u):
                dve.wait_ge(half_out, b + 1)
                dve.scalar_tensor_tensor(ot[:, :, bass.ds(b * N, N)],
                                         o_ps(u).rearrange("p (k t n) -> p k t n", k=DK, t=2)[:, :, 1, :],
                                         parity[:, 1:2], o_part[:, :, :], ALU.mult, ALU.add).then_inc(o_out, 1)

            def step(s, low, high, u):
                if high < B:
                    add_bias(s, u)
                    image_max(s, low, u)
                if low >= 1 and high <= B:
                    sums(s - 1, low - 1, (u + 1) % 2)
                if high < B:
                    less_max(s, low, u)
                if low >= 1 and high <= B:
                    inverse(s - 1, low - 1, (u + 1) % 2)
                if low >= 5 and high <= B + 4:
                    own_halves(s - 5, (u + 1) % 2)

            for s in range(8):
                step(s, s, s, s % 2)
            with dve.Fori(8, B - 3, 2) as s:
                for u in range(2):
                    step(s + u, 8, B - 3, u)

            def add_attended(i):
                n = TILES[i][1]
                dve.wait_ge(wo_done, i + 1)
                dve.tensor_tensor(h2[0:n, i, :], ps[0:n, PROJECT_BANK[i], 0:D], h1[0:n, i, :], ALU.add).then_inc(h2_ready, 1)
                dve.wait_ge(h2_ready, i + 1)
                moments(2, i, h2[0:n, i, :])

            def norm_second(i):
                turned, seen = (xn_turned, NT - 1 + i) if i < 1 else (x2_turned, i - 1)
                normed(2, i, TILES[i][1], 2 * NT + i + 1, h2[0:TILES[i][1], i, :], (NT + i) % 2, turned, seen)

            for s in range(B - 2, B + 5):
                step(s, s, s, s % 2)
                if s == B + 2:
                    dve.memset(gates[:, :, 0:E], 0.0)
                    chain(dve.memset(gates[:, :, E:E + TOP], -1.0))
                if s in PROJECT_AT:
                    add_attended(PROJECT_AT[s])
                if s in NORM_AT:
                    norm_second(NORM_AT[s])
            def second_low(i):
                turned_low(i, X_TURN_BANK[i], x2_hi, x2_lo)

            norm_second(2)
            second_low(0)
            attended_low(dve, NT - 1, o_lo_last)
            second_low(1)
            add_attended(3)
            second_low(2)
            add_attended(4)
            norm_second(3)
            norm_second(4)
            second_low(3)
            second_low(4)

            dve.wait_ge(gate_exp, 1)
            dve.tensor_scalar(gate_x[:, 0:NT - 1, :], gate_x[:, 0:NT - 1, :], 1.0, None, ALU.add)
            chain(dve.tensor_scalar(gate_x[0:LAST, NT - 1, :], gate_x[0:LAST, NT - 1, :], 1.0, None, ALU.add))
            dve.reciprocal(gates[:, 0:NT - 1, 0:E], gate_x[:, 0:NT - 1, :])
            chain(dve.reciprocal(gates[0:LAST, NT - 1, 0:E], gate_x[0:LAST, NT - 1, :]))
            for i in range(NT):
                last = dve.max(top8[:, i, :], gates[:, i, :])
            chain(last)
            chain(dve.memset(top8[:, :, TOP:8], -1.0))
            for i in range(NT):
                last = dve.match_replace(gates_rest[:, i, :], top8[:, i, :], gates[:, i, :], 0.0)
            chain(last)
            dve.tensor_tensor(gates_top[:, :, :], gates[:, :, 0:E], gates_rest[:, :, 0:E], ALU.subtract).then_inc(gate_top, 1)
            dve.wait_ge(gate_back, 1)
            dve.tensor_copy(gate_t[:, :], ps[:, 6:8, :].rearrange("p a n -> p (a n)")[0:E, 0:T]).then_inc(gate_out, 1)

            def apply_gate(e, low, u):
                dve.wait_ge(relu_done, e + 1)
                dve.wait_ge(g_landed[u % RING], 4 * e + (16 - 4 * (u % RING)))
                if low >= 2:
                    dve.wait_ge(h_lo, e - 1)
                dve.tensor_tensor(hg_f[:, u % 2, :], relu_h[:, u, :], gate_all[:, u % RING, :], ALU.mult).then_inc(gated, 1)

            def low_part(e, u):
                dve.wait_ge(h_hi, e + 1)
                dve.tensor_tensor(hs[1][:, u, :], hg_f[:, u % 2, :], f32(hs[0][:, u, :]), ALU.subtract).then_inc(h_lo, 1)

            apply_gate(0, 0, 0)
            apply_gate(1, 1, 1)
            low_part(0, 0)
            with dve.Fori(AHEAD, E - AHEAD + 1, AHEAD) as e:
                for u in range(AHEAD):
                    apply_gate(e + (u - 6), 2, (u + 2) % AHEAD)
                    low_part(e + (u - 7), (u + 1) % RING)
            for e in range(E, E + 7):
                if e - 6 < E:
                    apply_gate(e - 6, e - 6, (e - 6) % AHEAD)
                low_part(e - 7, (e - 7) % RING)
            for c in range(2):
                dve.wait_ge(experts_summed, c + 1)
                dve.tensor_copy(summed[:, 1, c * HALF:(c + 1) * HALF], down_ps(1, c)).then_inc(sum_kept_dve, 1)
            for i in range(0, NT - 1, 2):
                dve.wait_ge(sum_turned, i // 2 + 1)
                dve.tensor_tensor(h2[:, i:i + 2, :], ps[:, i // 2, :].rearrange("p (a d) -> p a d", a=2), h2[:, i:i + 2, :],
                                  ALU.add).then_inc(res_ready, 1)
            dve.wait_ge(sum_turned, (NT + 1) // 2)
            dve.tensor_tensor(h2[0:LAST, NT - 1, :], sum_turned_ps(NT - 1)[0:LAST], h2[0:LAST, NT - 1, :],
                              ALU.add).then_inc(res_ready, 1)

        @block.gpsimd
        def _(pool):
            count = [0]

            def chain(ins):
                count[0] += 1
                ins.then_inc(pool_step, 1)
                pool.wait_ge(pool_step, count[0])

            chain(pool.memset(ident[:, :], 0.0))
            pool.affine_select(out=ident[:, :], in_=ident[:, :], compare_op=ALU.not_equal, fill=1.0, base=0,
                               pattern=[[-1, P]], channel_multiplier=1).then_inc(const_done, 2)
            chain(pool.memset(f32(pick[:, :, :]), 0.0))
            pool.affine_select(out=pick[:, :, :], in_=f32(pick[:, :, :]), compare_op=ALU.not_equal, fill=1.0, base=0,
                               pattern=[[0, B], [-1, N]], channel_multiplier=1).then_inc(const_done, 1)
            chain(pool.memset(head_mask[:, :], 1.0))
            chain(pool.affine_select(out=head_mask[:, :], in_=head_mask[:, :], compare_op=ALU.is_ge, fill=0.0, base=0,
                                     pattern=[[-HD, HH]], channel_multiplier=1))
            pool.affine_select(out=head_mask[:, :], in_=head_mask[:, :], compare_op=ALU.is_ge, fill=0.0, base=HD - 1,
                               pattern=[[HD, HH]], channel_multiplier=-1).then_inc(const_done, 1)
            pool.iota(dist_i[:, :], pattern=[[1, N]], base=0, channel_multiplier=-1).then_inc(const_done, 1)
            pool.memset(neg_half[:, :], -0.5).then_inc(const_done, 1)

            pool.wait_ge(cls_landed, 16)
            pool.wait_ge(bias_landed, 16)
            pool.wait_ge(pos_landed, 16)
            chain(pool.tensor_copy(bias_rows[0:1, :], first_rows[0:1, :]))
            chain(pool.tensor_tensor(pos_b[:, :], pos_b[:, :], bias_rows[:, :], ALU.add))
            chain(pool.tensor_copy(pos_split[0][:, :], pos_b[:, :]))
            pool.tensor_tensor(pos_split[1][:, :], pos_b[:, :], f32(pos_split[0][:, :]), ALU.subtract).then_inc(pos_ready, 1)
            low_of_embedding(pool, 2, wt_lo_pool)

            def inverse_std(which, i, n, seen):
                pool.wait_ge(var_ready, seen)
                chain(pool.tensor_scalar(veps[0:n, which, i:i + 1], mv[0:n, which, i, 1:2], EPS, None, ALU.add))
                pool.tensor_tensor(rstd[0:n, which, i:i + 1], veps[0:n, which, i:i + 1], neg_half[0:n, :],
                                   ALU.pow).then_inc(rstd_ready, 1)

            for m in range(1, len(W_ORDER), 2):
                low_of_weights(pool, m, w_lo_pool)
            def rest_of_keys(e, u):
                pool.wait_ge(ek_hi, e + 1)
                pool.tensor_tensor(ek[1][:, u], raw_k[:, u, :].rearrange("p (k f) -> p k f", k=DK), f32(ek[0][:, u]),
                                   ALU.subtract).then_inc(k_split, 1)

            def rest_of_values(e, u):
                pool.wait_ge(ev_hi, e + 1)
                pool.tensor_tensor(ev[1][:, u], raw_v[:, u], f32(ev[0][:, u]), ALU.subtract).then_inc(v_split, 1)

            for seen, (which, i) in enumerate(MOMENTS_ORDER):
                inverse_std(which, i, TILES[i][1], seen + 1)
                if 1 <= seen <= 2 * RING:
                    (rest_of_keys, rest_of_values)[(seen - 1) % 2]((seen - 1) // 2, (seen - 1) // 2)
            pool.wait_ge(qk_out, DK)

            def mask_queries(b, low, u):
                if low >= 2:
                    pool.wait_ge(s_done, b - 1)
                q3 = qt[:, :, bass.ds(b * N, N)].rearrange("p k (o n) -> p k o n", o=1).to_broadcast([P, DK, HH, N])
                m3 = head_mask[:, :].rearrange("p (a h o) -> p a h o", a=1, o=1).to_broadcast([P, DK, HH, N])
                own = q_now[:, u].rearrange("p (k c) -> p k c", k=DK)[:, :, 0:HQ]
                pool.tensor_tensor(own.rearrange("p k (h n) -> p k h n", n=N), q3, m3, ALU.mult).then_inc(q_masked, 1)

            def scale_probs(b, low, u):
                pool.wait_ge(inv_done, b + 1)
                if low >= 2:
                    pool.wait_ge(p_turned, b - 1)
                pool.tensor_tensor(probs_n[:, u, :].rearrange("p (g n) -> p g n", n=N),
                                   probs[:, u, :].rearrange("p (g n) -> p g n", n=N),
                                   row_inv[:, u, :].rearrange("p (g o) -> p g o", o=1).to_broadcast([P, 2 * NT, N]),
                                   ALU.mult).then_inc(p_scaled, 1)

            def step(s, low, high, u):
                if low >= 2 and high <= B + 1:
                    scale_probs(s - 2, low - 2, u)
                if high + 2 < B:
                    mask_queries(s + 2, low + 2, u)

            pool.memset(q_now[:, :, HQ:HQ + P], 0.0)
            mask_queries(0, 0, 0)
            mask_queries(1, 1, 1)
            for s in range(8):
                if s + 2 == BHALF:
                    pool.wait_ge(qk_out, 3 * DK + DK)
                step(s, s, s, s % 2)
            with pool.Fori(8, B - 3, 2) as s:
                for u in range(2):
                    step(s + u, 8, B - 3, u)
            for s in range(B - 2, B + 2):
                step(s, s, s, s % 2)
                if s in O_LOW_AT:
                    attended_low(pool, O_LOW_AT[s], o_lo)
            for i in range(NT):
                inverse_std(2, i, TILES[i][1], 2 * NT + i + 1)
                if i in (0, 2):
                    attended_low(pool, 2 + i // 2, o_lo)
            for e in range(RING, AHEAD + 3):
                rest_of_keys(e, e % RING)
            with pool.Fori(AHEAD, E - 2 * RING + 1, RING) as e:
                for u in range(RING):
                    rest_of_keys(e + (u + 3), (u + 3) % RING)
                    rest_of_values(e + (u - RING), u)
            for e in range(E - RING, E + RING):
                if e + 3 < E:
                    rest_of_keys(e + 3, (e + 3) % RING)
                rest_of_values(e - RING, e % RING)


_INS = ['x', 'L0_tok_W', 'L0_tok_b', 'L0_tok_cls_token', 'L0_tok_pos_embedding', 'L0_tok_gamma', 'L0_tok_beta',
        'L0_attn_Wq', 'L0_attn_Wkv_short', 'L0_attn_Wkv_long', 'L0_attn_Wo', 'L0_attn_mix_weight',
        'L0_attn_decay_factor', 'L0_ffn_expert_sel', 'L0_ffn_keys', 'L0_ffn_values']


def kernel(**inputs):
    import numpy as _np
    import concourse.bacc as _bacc
    from concourse import mybir as _mybir
    from concourse.bass_utils import run_bass_kernel_spmd as _run

    nc = _bacc.Bacc("TRN2", target_bir_lowering=False, num_devices=1)
    arrays, args = {}, []
    for name in _INS:
        a = _np.ascontiguousarray(inputs[name])
        arrays[f"in_{name}_dram"] = a
        args.append(nc.dram_tensor(f"in_{name}_dram", a.shape, _mybir.dt.from_np(a.dtype), kind="ExternalInput").ap())
    batch, _, side, _ = inputs["x"].shape
    rows = inputs["L0_tok_pos_embedding"].shape[1]
    width = inputs["L0_tok_W"].shape[1]
    out = nc.dram_tensor("out_dram", (batch * rows, width), _mybir.dt.from_np(_np.dtype("float32")), kind="ExternalOutput").ap()
    vit_tower(nc, *args, out)
    r = _run(nc, [arrays], core_ids=[0])
    return r.results[0]["out_dram"].reshape(batch, rows, width)
```
